# Optimizing a Trainium2 kernel written in Bass

```python
import numpy as np
import jax
import jax.numpy as jnp

def _softmax(x, axis=-1):
    return jax.nn.softmax(x, axis=axis)

def _gelu(x):
    return jax.nn.gelu(x, approximate=True)

def _silu(x):
    return jax.nn.silu(x)

def _sigmoid(x):
    return jax.nn.sigmoid(x)

def _layernorm(x, axis=-1, eps=1e-05):
    m = jnp.mean(x, axis=axis, keepdims=True)
    v = jnp.var(x, axis=axis, keepdims=True)
    return (x - m) / jnp.sqrt(v + eps)

def _scatter_add(tgt, idx, src, axis=0):
    return tgt.at[idx].add(src)

def _segment_sum(src, seg, n):
    return jax.ops.segment_sum(src, seg, n)
kernel_name = 'mk_gnn_ffn_d2_gnn_r8_eb883c'

def setup_inputs(seed: int=0):
    np.random.seed(seed)
    _w = jnp.asarray

    def _rec_inputs():
        import jax
        import jax.numpy as jnp
        _gk = jax.random.key(seed)
        x = -0.0003713 + 1 * jax.random.normal(jax.random.fold_in(_gk, 1), (6250, 256), jnp.float32)
        _s = jax.random.randint(jax.random.fold_in(_gk, 2), (50000,), 0, 6250, jnp.int32)
        _d = jax.random.randint(jax.random.fold_in(_gk, 3), (50000,), 0, 6250, jnp.int32)
        _loop = jnp.arange(6250, dtype=jnp.int32)
        src = jnp.concatenate([_s, _d, _loop])
        dst = jnp.concatenate([_d, _s, _loop])
        _o = jnp.argsort(dst, stable=True)
        src = src[_o]
        dst = dst[_o]
        return (x, src, dst)
    x, src, dst = _rec_inputs()

    def _L0_gnn_setup():
        import jax, jax.numpy as jnp
        import numpy as np
        N = 6250
        E = 100000
        IN_DIM = 256
        HID = 128
        HEADS = 2
        OUT_DIM = 256
        NEG_SLOPE = 0.2

        def gat_layer(x, W, a_l, a_r, b, src, dst, num_nodes):
            heads, d = a_l.shape
            z = (x @ W).reshape(num_nodes, heads, d)
            el = jnp.einsum('nhd,hd->nh', z, a_l)
            er = jnp.einsum('nhd,hd->nh', z, a_r)
            e = el[src] + er[dst]
            e = jnp.where(e > 0, e, NEG_SLOPE * e)
            m = jax.ops.segment_max(e, dst, num_segments=num_nodes)
            ex = jnp.exp(e - m[dst])
            s = jax.ops.segment_sum(ex, dst, num_segments=num_nodes)
            alpha = ex / s[dst]
            msg = z[src] * alpha[:, :, None]
            out = jax.ops.segment_sum(msg, dst, num_segments=num_nodes)
            return out + b[None, :, :]
        key = jax.random.key(seed)
        ks = jax.random.split(key, 12)
        sc1 = 1.0 / np.sqrt(IN_DIM)
        sc2 = 1.0 / np.sqrt(HEADS * HID)
        return {'node_feats': jax.random.normal(ks[0], (N, IN_DIM), dtype=jnp.float32), 'src': jax.random.randint(ks[1], (E,), 0, N, dtype=jnp.int32), 'dst': jax.random.randint(ks[2], (E,), 0, N, dtype=jnp.int32), 'W1': jax.random.normal(ks[3], (IN_DIM, HEADS * HID), dtype=jnp.float32) * sc1, 'al1': jax.random.normal(ks[4], (HEADS, HID), dtype=jnp.float32) * sc1, 'ar1': jax.random.normal(ks[5], (HEADS, HID), dtype=jnp.float32) * sc1, 'b1': jnp.zeros((HEADS, HID), dtype=jnp.float32), 'W2': jax.random.normal(ks[6], (HEADS * HID, OUT_DIM), dtype=jnp.float32) * sc2, 'al2': jax.random.normal(ks[7], (1, OUT_DIM), dtype=jnp.float32) * sc2, 'ar2': jax.random.normal(ks[8], (1, OUT_DIM), dtype=jnp.float32) * sc2, 'b2': jnp.zeros((1, OUT_DIM), dtype=jnp.float32)}
    _L0_gnn_all = _L0_gnn_setup()
    _L0_gnn_in = {k: v for k, v in _L0_gnn_all.items() if k in ('W1', 'al1', 'ar1', 'b1', 'W2', 'al2', 'ar2', 'b2')}
    del _L0_gnn_all

    def _L0_ffn_setup():
        import jax, jax.numpy as jnp
        import numpy as np
        DIM = 256
        H = 8
        D = 64
        G = 64
        INNER = H * D
        SCALE = D ** (-0.5)
        key = jax.random.key(seed)
        ks = jax.random.split(key, 12)
        B, N = (4, 2048)
        x = jax.random.normal(ks[0], (B, N, DIM), dtype=jnp.float32)
        s = lambda fan_in: 1.0 / np.sqrt(fan_in)
        W_fx = jax.random.normal(ks[1], (DIM, INNER), dtype=jnp.float32) * s(DIM)
        b_fx = jnp.zeros((INNER,), dtype=jnp.float32)
        W_x = jax.random.normal(ks[2], (DIM, INNER), dtype=jnp.float32) * s(DIM)
        b_x = jnp.zeros((INNER,), dtype=jnp.float32)
        A = jax.random.normal(ks[3], (G, D), dtype=jnp.float32)
        Q, _ = jnp.linalg.qr(A.T)
        W_slice = Q[:, :G].astype(jnp.float32)
        b_slice = jnp.zeros((G,), dtype=jnp.float32)
        W_q = jax.random.normal(ks[4], (D, D), dtype=jnp.float32) * s(D)
        W_k = jax.random.normal(ks[5], (D, D), dtype=jnp.float32) * s(D)
        W_v = jax.random.normal(ks[6], (D, D), dtype=jnp.float32) * s(D)
        W_out = jax.random.normal(ks[7], (INNER, DIM), dtype=jnp.float32) * s(INNER)
        b_out = jnp.zeros((DIM,), dtype=jnp.float32)
        temperature = jnp.ones((1, H, 1, 1), dtype=jnp.float32) * 0.5
        return {'x': x, 'W_fx': W_fx, 'b_fx': b_fx, 'W_x': W_x, 'b_x': b_x, 'W_slice': W_slice, 'b_slice': b_slice, 'W_q': W_q, 'W_k': W_k, 'W_v': W_v, 'W_out': W_out, 'b_out': b_out, 'temperature': temperature}
    _L0_ffn_all = _L0_ffn_setup()
    _L0_ffn_in = {k: v for k, v in _L0_ffn_all.items() if k in ('W_fx', 'b_fx', 'W_x', 'b_x', 'W_slice', 'b_slice', 'W_q', 'W_k', 'W_v', 'W_out', 'b_out', 'temperature')}
    del _L0_ffn_all

    def _L1_gnn_setup():
        import jax, jax.numpy as jnp
        import numpy as np
        N = 12500
        E = 200000
        D = 256
        BN_EPS = 1e-05

        def _batchnorm(x, gamma, beta):
            mu = jnp.mean(x, axis=0)
            var = jnp.var(x, axis=0)
            return (x - mu) * jax.lax.rsqrt(var + BN_EPS) * gamma + beta

        def _gin_conv(x, src, dst, n, W1, b1, gamma, beta, W2, b2):
            agg = jax.ops.segment_sum(x[src], dst, num_segments=n)
            h = x + agg
            h = jax.nn.relu(_batchnorm(h @ W1 + b1, gamma, beta))
            return jax.nn.relu(h @ W2 + b2)
        key = jax.random.key(seed)
        ks = jax.random.split(key, 8)
        x = jax.random.normal(ks[0], (N, D), dtype=jnp.float32)
        edge_index = jax.random.randint(ks[1], (2, E), 0, N, dtype=jnp.int64)
        s = 0.02
        inp = {'x': x, 'edge_index': edge_index, 'g0': jnp.ones((D,), jnp.float32), 'b0': jnp.zeros((D,), jnp.float32), 'W1a': jax.random.normal(ks[2], (D, D), jnp.float32) * s, 'b1a': jnp.zeros((D,), jnp.float32), 'g1': jnp.ones((D,), jnp.float32), 'bt1': jnp.zeros((D,), jnp.float32), 'W1b': jax.random.normal(ks[3], (D, D), jnp.float32) * s, 'b1b': jnp.zeros((D,), jnp.float32), 'W2a': jax.random.normal(ks[4], (D, D), jnp.float32) * s, 'b2a': jnp.zeros((D,), jnp.float32), 'g2': jnp.ones((D,), jnp.float32), 'bt2': jnp.zeros((D,), jnp.float32), 'W2b': jax.random.normal(ks[5], (D, D), jnp.float32) * s, 'b2b': jnp.zeros((D,), jnp.float32)}
        return inp
    _L1_gnn_all = _L1_gnn_setup()
    _L1_gnn_in = {k: v for k, v in _L1_gnn_all.items() if k in ('g0', 'b0', 'W1a', 'b1a', 'g1', 'bt1', 'W1b', 'b1b', 'W2a', 'b2a', 'g2', 'bt2', 'W2b', 'b2b')}
    del _L1_gnn_all

    def _L1_ffn_setup():
        import jax, jax.numpy as jnp
        import numpy as np
        IN_CH = 256
        OUT_CH = 256
        key = jax.random.key(seed)
        kx, kw, kb = jax.random.split(key, 3)
        x = jax.random.normal(kx, (8, 512, IN_CH), dtype=jnp.float32)
        bound = 1.0 / np.sqrt(IN_CH)
        weight = jax.random.uniform(kw, (OUT_CH, IN_CH), dtype=jnp.float32, minval=-bound, maxval=bound)
        bias = jax.random.uniform(kb, (OUT_CH,), dtype=jnp.float32, minval=-bound, maxval=bound)
        return {'x': x, 'weight': weight, 'bias': bias}
    _L1_ffn_all = _L1_ffn_setup()
    _L1_ffn_in = {k: v for k, v in _L1_ffn_all.items() if k in ('weight', 'bias')}
    del _L1_ffn_all
    return {'x': x, 'src': src, 'dst': dst, 'L0_gnn_W1': _L0_gnn_in['W1'], 'L0_gnn_al1': _L0_gnn_in['al1'], 'L0_gnn_ar1': _L0_gnn_in['ar1'], 'L0_gnn_b1': _L0_gnn_in['b1'], 'L0_gnn_W2': _L0_gnn_in['W2'], 'L0_gnn_al2': _L0_gnn_in['al2'], 'L0_gnn_ar2': _L0_gnn_in['ar2'], 'L0_gnn_b2': _L0_gnn_in['b2'], 'L0_ffn_W_fx': _L0_ffn_in['W_fx'], 'L0_ffn_b_fx': _L0_ffn_in['b_fx'], 'L0_ffn_W_x': _L0_ffn_in['W_x'], 'L0_ffn_b_x': _L0_ffn_in['b_x'], 'L0_ffn_W_slice': _L0_ffn_in['W_slice'], 'L0_ffn_b_slice': _L0_ffn_in['b_slice'], 'L0_ffn_W_q': _L0_ffn_in['W_q'], 'L0_ffn_W_k': _L0_ffn_in['W_k'], 'L0_ffn_W_v': _L0_ffn_in['W_v'], 'L0_ffn_W_out': _L0_ffn_in['W_out'], 'L0_ffn_b_out': _L0_ffn_in['b_out'], 'L0_ffn_temperature': _L0_ffn_in['temperature'], 'L1_gnn_g0': _L1_gnn_in['g0'], 'L1_gnn_b0': _L1_gnn_in['b0'], 'L1_gnn_W1a': _L1_gnn_in['W1a'], 'L1_gnn_b1a': _L1_gnn_in['b1a'], 'L1_gnn_g1': _L1_gnn_in['g1'], 'L1_gnn_bt1': _L1_gnn_in['bt1'], 'L1_gnn_W1b': _L1_gnn_in['W1b'], 'L1_gnn_b1b': _L1_gnn_in['b1b'], 'L1_gnn_W2a': _L1_gnn_in['W2a'], 'L1_gnn_b2a': _L1_gnn_in['b2a'], 'L1_gnn_g2': _L1_gnn_in['g2'], 'L1_gnn_bt2': _L1_gnn_in['bt2'], 'L1_gnn_W2b': _L1_gnn_in['W2b'], 'L1_gnn_b2b': _L1_gnn_in['b2b'], 'L1_ffn_weight': _L1_ffn_in['weight'], 'L1_ffn_bias': _L1_ffn_in['bias']}

def reference(x, src, dst, L0_gnn_W1, L0_gnn_al1, L0_gnn_ar1, L0_gnn_b1, L0_gnn_W2, L0_gnn_al2, L0_gnn_ar2, L0_gnn_b2, L0_ffn_W_fx, L0_ffn_b_fx, L0_ffn_W_x, L0_ffn_b_x, L0_ffn_W_slice, L0_ffn_b_slice, L0_ffn_W_q, L0_ffn_W_k, L0_ffn_W_v, L0_ffn_W_out, L0_ffn_b_out, L0_ffn_temperature, L1_gnn_g0, L1_gnn_b0, L1_gnn_W1a, L1_gnn_b1a, L1_gnn_g1, L1_gnn_bt1, L1_gnn_W1b, L1_gnn_b1b, L1_gnn_W2a, L1_gnn_b2a, L1_gnn_g2, L1_gnn_bt2, L1_gnn_W2b, L1_gnn_b2b, L1_ffn_weight, L1_ffn_bias):
    import jax
    import jax.numpy as jnp

    def _L0_gnn_ref(node_feats, src, dst, W1, al1, ar1, b1, W2, al2, ar2, b2):
        import jax, jax.numpy as jnp
        import numpy as np
        N = 6250
        E = 100000
        IN_DIM = 256
        HID = 128
        HEADS = 2
        OUT_DIM = 256
        NEG_SLOPE = 0.2

        def gat_layer(x, W, a_l, a_r, b, src, dst, num_nodes):
            heads, d = a_l.shape
            z = (x @ W).reshape(num_nodes, heads, d)
            el = jnp.einsum('nhd,hd->nh', z, a_l)
            er = jnp.einsum('nhd,hd->nh', z, a_r)
            e = el[src] + er[dst]
            e = jnp.where(e > 0, e, NEG_SLOPE * e)
            m = jax.ops.segment_max(e, dst, num_segments=num_nodes)
            ex = jnp.exp(e - m[dst])
            s = jax.ops.segment_sum(ex, dst, num_segments=num_nodes)
            alpha = ex / s[dst]
            msg = z[src] * alpha[:, :, None]
            out = jax.ops.segment_sum(msg, dst, num_segments=num_nodes)
            return out + b[None, :, :]
        h = gat_layer(node_feats, W1, al1, ar1, b1, src, dst, N)
        h = jax.nn.relu(h.reshape(N, HEADS * HID))
        out = gat_layer(h, W2, al2, ar2, b2, src, dst, N)
        return out[:, 0, :]

    def _L0_ffn_ref(x, W_fx, b_fx, W_x, b_x, W_slice, b_slice, W_q, W_k, W_v, W_out, b_out, temperature):
        import jax, jax.numpy as jnp
        import numpy as np
        DIM = 256
        H = 8
        D = 64
        G = 64
        INNER = H * D
        SCALE = D ** (-0.5)
        B, N, _ = x.shape
        fx_mid = (x @ W_fx + b_fx).reshape(B, N, H, D).transpose(0, 2, 1, 3)
        x_mid = (x @ W_x + b_x).reshape(B, N, H, D).transpose(0, 2, 1, 3)
        temp = jnp.clip(temperature, 0.1, 5.0)
        slice_weights = jax.nn.softmax((x_mid @ W_slice + b_slice) / temp, axis=-1)
        slice_norm = slice_weights.sum(axis=2)
        slice_token = jnp.einsum('bhnc,bhng->bhgc', fx_mid, slice_weights)
        slice_token = slice_token / (slice_norm[..., None] + 1e-05)
        q = slice_token @ W_q
        k = slice_token @ W_k
        v = slice_token @ W_v
        attn = jax.nn.softmax(jnp.einsum('bhgc,bhkc->bhgk', q, k) * SCALE, axis=-1)
        out_slice = jnp.einsum('bhgk,bhkc->bhgc', attn, v)
        out_x = jnp.einsum('bhgc,bhng->bhnc', out_slice, slice_weights)
        out_x = out_x.transpose(0, 2, 1, 3).reshape(B, N, INNER)
        return out_x @ W_out + b_out

    def _L1_gnn_ref(x, edge_index, g0, b0, W1a, b1a, g1, bt1, W1b, b1b, W2a, b2a, g2, bt2, W2b, b2b):
        import jax, jax.numpy as jnp
        import numpy as np
        N = 12500
        E = 200000
        D = 256
        BN_EPS = 1e-05

        def _batchnorm(x, gamma, beta):
            mu = jnp.mean(x, axis=0)
            var = jnp.var(x, axis=0)
            return (x - mu) * jax.lax.rsqrt(var + BN_EPS) * gamma + beta

        def _gin_conv(x, src, dst, n, W1, b1, gamma, beta, W2, b2):
            agg = jax.ops.segment_sum(x[src], dst, num_segments=n)
            h = x + agg
            h = jax.nn.relu(_batchnorm(h @ W1 + b1, gamma, beta))
            return jax.nn.relu(h @ W2 + b2)
        n = x.shape[0]
        src, dst = (edge_index[0], edge_index[1])
        h = _batchnorm(x, g0, b0)
        h = _gin_conv(h, src, dst, n, W1a, b1a, g1, bt1, W1b, b1b)
        h = jax.nn.relu(h)
        h = _gin_conv(h, src, dst, n, W2a, b2a, g2, bt2, W2b, b2b)
        return jax.nn.relu(h)

    def _L1_ffn_ref(x, weight, bias):
        import jax, jax.numpy as jnp
        import numpy as np
        IN_CH = 256
        OUT_CH = 256
        return jnp.einsum('bsi,oi->bso', x, weight) + bias
    edge_index = jnp.stack([src, dst])
    x = x + _L0_gnn_ref(_layernorm(x, axis=-1), src, dst, L0_gnn_W1, L0_gnn_al1, L0_gnn_ar1, L0_gnn_b1, L0_gnn_W2, L0_gnn_al2, L0_gnn_ar2, L0_gnn_b2)
    x = x + _L0_ffn_ref(_layernorm(x, axis=-1)[None], L0_ffn_W_fx, L0_ffn_b_fx, L0_ffn_W_x, L0_ffn_b_x, L0_ffn_W_slice, L0_ffn_b_slice, L0_ffn_W_q, L0_ffn_W_k, L0_ffn_W_v, L0_ffn_W_out, L0_ffn_b_out, L0_ffn_temperature)[0]
    x = x + _L1_gnn_ref(_layernorm(x, axis=-1), edge_index, L1_gnn_g0, L1_gnn_b0, L1_gnn_W1a, L1_gnn_b1a, L1_gnn_g1, L1_gnn_bt1, L1_gnn_W1b, L1_gnn_b1b, L1_gnn_W2a, L1_gnn_b2a, L1_gnn_g2, L1_gnn_bt2, L1_gnn_W2b, L1_gnn_b2b)
    x = x + _L1_ffn_ref(_layernorm(x, axis=-1)[None], L1_ffn_weight, L1_ffn_bias)[0]
    return x

_drawn_inputs = setup_inputs


def setup_inputs(seed=0):
    import zlib

    import numpy as np

    out = dict(_drawn_inputs(seed))
    spreads = {'L0_gnn_b1': (0.0, 0.1),
     'L0_gnn_b2': (0.0, 0.1),
     'L0_ffn_b_fx': (0.0, 0.1),
     'L0_ffn_b_x': (0.0, 0.8),
     'L0_ffn_b_slice': (0.0, 0.8),
     'L0_ffn_b_out': (0.0, 0.1),
     'L0_ffn_temperature': (0.5, 0.6),
     'L1_gnn_g0': (1.0, 0.55),
     'L1_gnn_b0': (0.0, 0.686),
     'L1_gnn_b1a': (0.0, 2.0),
     'L1_gnn_g1': (1.0, 0.2),
     'L1_gnn_bt1': (0.0, 0.588),
     'L1_gnn_b1b': (0.0, 0.1),
     'L1_gnn_b2a': (0.0, 2.0),
     'L1_gnn_g2': (1.0, 0.2),
     'L1_gnn_bt2': (0.0, 0.509),
     'L1_gnn_b2b': (0.0, 0.1)}
    factors = {'L0_gnn_ar1': 7.565,
     'L0_gnn_al2': 8.0,
     'L0_gnn_ar2': 8.0,
     'L0_ffn_W_x': 8.0,
     'L0_ffn_W_slice': 8.0,
     'L0_ffn_W_q': 8.0,
     'L0_ffn_W_k': 8.0}
    for name, (base, spread) in spreads.items():
        noise = np.random.default_rng([zlib.crc32(name.encode()), seed]).standard_normal(out[name].shape)
        drawn = base * np.exp(spread * noise) if base else spread * noise
        out[name] = jnp.asarray(drawn.astype(out[name].dtype))
    for name, factor in factors.items():
        out[name] = (out[name] * factor).astype(out[name].dtype)
    return out
```

```python
import numpy as np
from contextlib import ExitStack

import concourse.bass as bass
from concourse import mybir

F32 = mybir.dt.float32
BF16 = mybir.dt.bfloat16
I32 = mybir.dt.int32
ALU = mybir.AluOpType
ACT = mybir.ActivationFunctionType
AX = mybir.AxisListType

N = 6250
D = 256
E = 106250
P = 128
NB = -(-N // P)
TAIL = N - (NB - 1) * P
NPAD = NB * P
EP, EC = 125, 850
ET = EC
EPAD = ET * P - E
PADP, PADC = 102, 25
GS = 8
NG = -(-(-(-E // P) + NB) // GS)
RING = 4
TC = -(-NG * GS // P)
SK = TC * P
H1 = 2
HD = D // H1
ROW1 = D + 2 * H1
ROW2 = D + 2
ACW = D + H1
FAR = 1.0e30
EPS = 1e-5
SLOPE = 0.2
NH, DH, NSL = 8, 64, 64
INNER = NH * DH
ARENA = 25700
AGG0 = ARENA - NB * ACW
PAD_DST = 1 << 20


def unrolled(eng, total, unroll, body, head, tail):
    turns = (total - head - tail) // unroll
    for s in range(head):
        body(s, s % unroll, s // unroll)
    if turns > 0:
        assert head % unroll == 0
        with eng.Fori(head // unroll, head // unroll + turns) as it:
            for c in range(unroll):
                body(it * unroll + c, c, it)
    for s in range(head + max(turns, 0) * unroll, total):
        body(s, s % unroll, s // unroll)


def turn(t, c, back, unroll):
    return t + (c - back) // unroll


def in_range(s, lo, hi):
    return not isinstance(s, int) or lo <= s < hi


def ge(eng, sem, value):
    if isinstance(value, int) and value <= 0:
        return
    eng.wait_ge(sem, value)


class Core:

    def __init__(self, nc, stack):
        self.nc, self.stack = nc, stack
        self.arena = self.sb("arena", [P, ARENA])
        self.work = self.sb("work", [P, RING * GS * ROW1])
        self.hot = self.sb("hot", [P, RING, GS * P])
        self.ident = self.sb("ident", [P, P])
        self.ones = self.sb("ones", [P, P])
        self.iota_col = self.sb("iota_col", [P, P])
        self.part = self.sb("part", [P, 1])
        self.step_idx = self.sb("step_idx", [P, SK], I32)
        self.step_dst = self.sb("step_dst", [P, SK])
        self.step_same = self.sb("step_same", [P, SK])
        self.step_reset = self.sb("step_reset", [P, SK])
        self.step_sel = self.sb("step_sel", [NB, SK])
        self.step_at = self.sb("step_at", [1, SK], I32)
        self.er = self.sb("er", [P, H1, NB])
        self.el = self.sb("el", [P, H1, NB])
        self.er_steps = self.sb("er_steps", [P, H1, SK])
        self.er_parts = self.sb("er_parts", [P, 3, H1, SK], BF16)
        self.low = self.sb("low", [P, 2])
        self.moments = self.sb("moments", [P, NB, 10])
        self.idx_ring = self.sb("idx_ring", [P, RING, GS], I32)
        self.psum = stack.enter_context(nc.psum_tensor("psum", [P, 4096], F32))
        self.dl_rows = nc.dram_tensor("dl_rows", (SK, P), BF16).ap()

    def sb(self, name, shape, dt=F32):
        return self.stack.enter_context(self.nc.sbuf_tensor(name, shape, dt))

    def bank(self, n, width=512):
        return self.psum[:, n * 512:n * 512 + width]

    def agg(self, b):
        return self.arena[:, AGG0 + b * ACW:AGG0 + (b + 1) * ACW]


def sems(nc, stack, names):
    made = [stack.enter_context(nc.semaphore(n)) for n in names.split()]
    start = made[0].num
    for before, after in zip(made, made[1:] + [None]):
        if after is None or after.num != before.num + 1:
            stack.callback(nc.gpsimd.sem_clear, range(start, before.num + 1))
            start = after.num if after is not None else 0
    return made


def ring_sems(nc, stack, name, count):
    return sems(nc, stack, " ".join(f"{name}{r}" for r in range(count)))


def set_constants(nc, core):
    with ExitStack() as st:
        zeroed, = sems(nc, st, "ident_zeroed")
        block = st.enter_context(nc.Block())

        @block.gpsimd
        def _(pool):
            nc.gpsimd.memset(core.ident[:], 0.0).then_inc(zeroed, 1)
            nc.gpsimd.iota(core.iota_col[:], pattern=[[1, P]], base=0, channel_multiplier=0,
                           allow_small_or_imprecise_dtypes=True)
            nc.gpsimd.iota(core.part[:], pattern=[[0, 1]], base=0, channel_multiplier=1,
                           allow_small_or_imprecise_dtypes=True)
            pool.wait_ge(zeroed, 1)
            nc.gpsimd.affine_select(out=core.ident[:], in_=core.ident[:], compare_op=ALU.not_equal, fill=1.0,
                                    base=0, pattern=[[-1, P]], channel_multiplier=1)

        @block.vector
        def _(dve):
            nc.vector.memset(core.ones[:], 1.0)
            nc.vector.memset(core.arena[:, AGG0:ARENA], 0.0)


def plan_steps(nc, core, src, dst):
    src_rows = nc.dram_tensor("src_rows", (ET, P), I32).ap()
    dst_rows = nc.dram_tensor("dst_rows", (ET, P), I32).ap()
    at = [0]

    def scratch(cols, dt=F32):
        view = core.arena[:, at[0]:at[0] + cols]
        at[0] += cols
        return view if dt == F32 else view.bitcast(dt)

    e_src, e_dst = scratch(EC, I32), scratch(EC, I32)
    blk_i, blk = scratch(EC, I32), scratch(EC // 2, BF16)
    less = scratch(EC // 2, BF16)
    pad = scratch(2 * PADC, I32)
    below = scratch(NB)
    bound, bound_i = scratch(1), scratch(1, I32)
    k_idx, reached, brow, trow = scratch(SK), scratch(SK), scratch(SK), scratch(SK)
    tile_i, blk_off = scratch(TC, I32), scratch(TC)
    g_src, g_dst = scratch(SK, I32), scratch(SK, I32)
    f_src, f_dst, b_dst = scratch(SK), scratch(SK), scratch(SK // 2, BF16)
    assert at[0] <= AGG0

    def flat(t, lo, hi, parts):
        return t.rearrange("r e -> (r e)")[lo:hi].rearrange("(p c) -> p c", p=parts)

    with ExitStack() as st:
        edges_in, pad_set, rows_out, counted = sems(nc, st, "edges_in pad_set rows_out counted")
        block = st.enter_context(nc.Block())

        @block.sync
        def _(sp):
            sp.dma_start(e_dst[0:EP, :], dst.rearrange("(p c) -> p c", p=EP)).then_inc(edges_in, 16)
            sp.dma_start(e_src[0:EP, :], src.rearrange("(p c) -> p c", p=EP)).then_inc(edges_in, 16)
            sp.wait_ge(edges_in, 32)
            sp.dma_start(flat(dst_rows, 0, E, EP), e_dst[0:EP, :]).then_inc(rows_out, 16)
            sp.dma_start(flat(src_rows, 0, E, EP), e_src[0:EP, :]).then_inc(rows_out, 16)
            sp.wait_ge(pad_set, 2)
            sp.dma_start(flat(dst_rows, E, ET * P, PADP), pad[0:PADP, 0:PADC]).then_inc(rows_out, 16)
            sp.dma_start(flat(src_rows, E, ET * P, PADP), pad[0:PADP, PADC:]).then_inc(rows_out, 16)
            sp.wait_ge(rows_out, 64)

        @block.gpsimd
        def _(pool):
            nc.gpsimd.memset(pad[:, 0:PADC], PAD_DST).then_inc(pad_set, 1)
            nc.gpsimd.memset(pad[:, PADC:], 0).then_inc(pad_set, 1)
            nc.gpsimd.iota(k_idx, pattern=[[1, SK]], base=0, channel_multiplier=0,
                           allow_small_or_imprecise_dtypes=True)

        @block.vector
        def _(dve):
            nc.vector.memset(below[:, 0:1], 0.0)
            dve.wait_ge(edges_in, 32)
            nc.vector.tensor_single_scalar(blk_i[0:EP, :], e_dst[0:EP, :], P.bit_length() - 1, ALU.arith_shift_right)
            dve.drain()
            nc.vector.tensor_copy(blk[0:EP, :], blk_i[0:EP, :])
            for b in range(1, NB):
                dve.drain()
                nc.vector.tensor_scalar(less[0:EP, :], blk[0:EP, :], float(b), 0.0, ALU.is_lt, ALU.add,
                                        accum_out=below[0:EP, b:b + 1])
            dve.drain()
            nc.vector.memset(bound, 0.0).then_inc(counted, 1)

        @block.tensor
        def _(pe):
            pe.wait_ge(counted, 1)
            nc.tensor.matmul(core.bank(0, 1)[0:NB, :], below[0:EP, 0:NB], core.ones[0:EP, 0:1], start=True, stop=True)

    with ExitStack() as st:
        reached_set, brow_summed = sems(nc, st, "reached_set brow_summed")
        block = st.enter_context(nc.Block())

        @block.vector
        def _(dve):
            nc.vector.tensor_copy(bound_i[0:NB, :], core.bank(0, 1)[0:NB, :])
            dve.drain()
            nc.vector.tensor_single_scalar(tile_i[0:NB, 0:1], bound_i[0:NB, :], P.bit_length() - 1, ALU.arith_shift_right)
            dve.drain()
            nc.vector.tensor_copy(blk_off[0:NB, 0:1], tile_i[0:NB, 0:1])
            dve.drain()
            nc.vector.tensor_tensor(bound[0:NB, :], blk_off[0:NB, 0:1], core.part[0:NB, :], ALU.add)
            dve.drain()
            nc.vector.tensor_scalar(reached[0:NB, :], k_idx[0:NB, :], bound[0:NB, 0:1], None, ALU.is_ge)\
                .then_inc(reached_set, 1)
            dve.wait_ge(brow_summed, 1)
            nc.vector.tensor_scalar(brow, core.psum[:, 512:512 + 2 * 512].rearrange("p (a k) -> p a k", a=2)
                                    [:, :, 0:SK // 2], -1.0, None, ALU.add)
            dve.drain()
            nc.vector.tensor_tensor(trow, k_idx, brow, ALU.subtract)
            nc.vector.tensor_tensor(core.step_same[:, 1:SK], brow[:, 1:SK], brow[:, 0:SK - 1], ALU.is_equal)
            nc.vector.memset(core.step_same[:, 0:1], 0.0)
            nc.vector.tensor_scalar(core.step_at[:], brow[0:1, :], float(ACW), float(AGG0), ALU.mult, ALU.add)
            nc.vector.tensor_scalar(core.step_sel[:], brow[0:NB, :], core.part[0:NB, 0:1], None, ALU.is_equal)
            dve.drain()
            nc.vector.tensor_scalar(core.step_reset[:], core.step_same[:], -1.0, FAR, ALU.add, ALU.mult)

        @block.tensor
        def _(pe):
            pe.wait_ge(reached_set, 1)
            for a in range(2):
                last = nc.tensor.matmul(core.bank(1 + a, SK // 2), core.ones[0:NB, :],
                                        reached[0:NB, a * (SK // 2):(a + 1) * (SK // 2)], start=True, stop=True)
            last.then_inc(brow_summed, 1)

    with ExitStack() as st:
        turned, tiles_set, shifted, flipped, kept = sems(nc, st, "turned tiles_set shifted flipped kept")
        rows_in = core.stack.enter_context(nc.semaphore("plan_rows_in"))
        block = st.enter_context(nc.Block())
        t_ps, b_ps = core.bank(0, TC), core.bank(1, TC)

        @block.tensor
        def _(pe):
            for c in range(TC):
                nc.tensor.matmul(t_ps[:, c:c + 1], trow[0:1, c * P:(c + 1) * P], core.ones[0:1, 0:1], start=True, stop=True)
                last = nc.tensor.matmul(b_ps[:, c:c + 1], brow[0:1, c * P:(c + 1) * P], core.ones[0:1, 0:1],
                                        start=True, stop=True)
            last.then_inc(turned, 1)
            pe.wait_ge(shifted, 1)
            for n, rows in enumerate((f_src, f_dst)):
                for c in range(TC):
                    last = nc.tensor.transpose(core.psum[:, (2 + 2 * n) * 512 + c * P:(2 + 2 * n) * 512 + (c + 1) * P],
                                               rows[:, c * P:(c + 1) * P], core.ident[:])
            last.then_inc(flipped, 1)

        @block.gpsimd
        def _(pool):
            pool.wait_ge(tiles_set, 1)
            pool.nop(nofuse=True)
            for c in range(TC):
                for rows, table in ((g_src, src_rows), (g_dst, dst_rows)):
                    nc.gpsimd.indirect_dma_start(
                        rows[:, c * P:(c + 1) * P], None, table,
                        bass.IndirectOffsetOnAxis(ap=tile_i[:, c:c + 1], axis=0)).then_inc(rows_in, 16)

        @block.vector
        def _(dve):
            dve.wait_ge(turned, 1)
            nc.vector.tensor_copy(tile_i[:, 0:TC], t_ps).then_inc(tiles_set, 1)
            nc.vector.tensor_scalar(blk_off[:, 0:TC], b_ps, float(P), None, ALU.mult)
            dve.wait_ge(rows_in, 32 * TC)
            nc.vector.tensor_copy(f_src, g_src)
            nc.vector.tensor_copy(f_dst, g_dst)
            dve.drain()
            for c in range(TC):
                nc.vector.tensor_scalar(f_dst[:, c * P:(c + 1) * P], f_dst[:, c * P:(c + 1) * P],
                                        blk_off[:, c:c + 1], None, ALU.subtract)
            dve.drain()
            nc.vector.tensor_copy(b_dst, f_dst).then_inc(shifted, 1)
            dve.wait_ge(flipped, 1)
            nc.vector.tensor_copy(core.step_idx[:], core.psum[:, 2 * 512:2 * 512 + SK])
            nc.vector.tensor_copy(core.step_dst[:], core.psum[:, 4 * 512:4 * 512 + SK])

        @block.sync
        def _(sp):
            sp.wait_ge(shifted, 1)
            sp.dma_start(core.dl_rows.rearrange("(c p) e -> p c e", p=P),
                         b_dst.rearrange("p (c e) -> p c e", e=P)).then_inc(kept, 16)
            sp.wait_ge(kept, 16)


def dense_tiles(nc, name, core, weights, cols, load, prepare, finish, store, func=ACT.Copy):
    lhs = core.work[:, 0:2 * D].rearrange("p (r c f) -> p r c f", r=2, c=2)
    turned = core.work[:, 2 * D:4 * D].rearrange("p (r c f) -> p r c f", r=2, c=2)
    with ExitStack() as st:
        tile_set, tile_turned, tile_copied, product, product_used, load_free = sems(
            nc, st, " ".join(f"{name}_{x}" for x in
                             "tile tile_turned tile_copied product product_used load_free".split()))
        stored, loaded = (ring_sems(nc, st, f"{name}_{x}", 2) for x in ("stored", "loaded"))
        block = st.enter_context(nc.Block())

        @block.vector
        def _(dve):
            def slot(s, c, t):
                if in_range(s, 0, NB):
                    if load is not None:
                        dve.wait_ge(loaded[c % 2], (t + 1) * 16)
                    ge(dve, tile_turned, s - 1)
                    prepare(dve, s, lhs[:, c % 2].rearrange("p c f -> p (c f)"), c % 2, load_free).then_inc(tile_set, 1)
                if in_range(s, 1, NB + 1):
                    dve.wait_ge(product, s)
                    if store is not None:
                        ge(dve, stored[(c + 1) % 2], turn(t, c, 1, 2) * 16)
                    finish(dve, s - 1, core.bank(4 + (c + 1) % 2, cols), (c + 1) % 2).then_inc(product_used, 1)
            unrolled(dve, NB + 1, 2, slot, 2, 2)

        @block.tensor
        def _(pe):
            def slot(s, c, t):
                if in_range(s, 0, NB):
                    pe.wait_ge(tile_set, s + 1)
                    ge(pe, tile_copied, s - 1)
                    for k in range(2):
                        last = nc.tensor.transpose(core.psum[:, (c % 2) * 512 + k * P:(c % 2) * 512 + (k + 1) * P],
                                                   lhs[:, c % 2, k], core.ident[:])
                    last.then_inc(tile_turned, 1)
                if in_range(s, 1, NB + 1):
                    pe.wait_ge(tile_copied, s)
                    ge(pe, product_used, s - 2)
                    for k in range(2):
                        last = nc.tensor.matmul(core.bank(4 + (c + 1) % 2, cols), turned[:, (c + 1) % 2, k], weights[k],
                                                start=(k == 0), stop=(k == 1))
                    last.then_inc(product, 1)
            unrolled(pe, NB + 1, 2, slot, 2, 2)

        @block.scalar
        def _(act):
            def slot(s, c, t):
                act.wait_ge(tile_turned, s + 1)
                ge(act, product, s - 1)
                nc.scalar.activation(turned[:, c % 2].rearrange("p c f -> p (c f)"),
                                     core.psum[:, (c % 2) * 512:(c % 2) * 512 + D], func).then_inc(tile_copied, 1)
            unrolled(act, NB, 2, slot, 2, 2)

        @block.sync
        def _(sp):
            def slot(s, c, t):
                if load is not None:
                    if in_range(s, 0, NB):
                        ge(sp, load_free, s - 1)
                        load(sp, s, c % 2).then_inc(loaded[c % 2], 16)
                if store is not None and in_range(s, 1, NB + 1):
                    sp.wait_ge(product_used, s)
                    store(sp, s - 1, (c + 1) % 2).then_inc(stored[(c + 1) % 2], 16)
            if load is not None or store is not None:
                unrolled(sp, NB + 1, 2, slot, 2, 2)
            if store is not None:
                for r in range(2):
                    sp.wait_ge(stored[r], 16 * ((NB + 1 - r) // 2))


def row_moments(nc, core, name, steps, rows):
    six = core.moments[:, :, 3:9]
    with ExitStack() as st:
        moments_set, rooted = sems(nc, st, f"{name}_moments {name}_rooted")
        block = st.enter_context(nc.Block())

        @block.vector
        def _(dve):
            last = len(steps)

            def slot(s, c, t):
                for n, step in enumerate(steps):
                    if in_range(s, n, NB + n):
                        step(dve, s - n, c)
                if in_range(s, last, NB + last):
                    nc.vector.bn_stats(six[:, bass.ds(s - last, 1)].rearrange("p o n -> p (o n)"), rows(s - last))
                if steps:
                    dve.drain()
            unrolled(dve, NB + last, 2, slot, 2, 3)
            dve.drain()
            m = core.moments
            half_diff = m[:, :, 9:10]
            nc.vector.tensor_tensor(m[:, :, 0:1], m[:, :, 4:5], m[:, :, 7:8], ALU.add)
            nc.vector.tensor_tensor(half_diff, m[:, :, 4:5], m[:, :, 7:8], ALU.subtract)
            nc.vector.tensor_tensor(m[:, :, 1:2], m[:, :, 5:6], m[:, :, 8:9], ALU.add)
            dve.drain()
            nc.vector.tensor_scalar(m[:, :, 0:1], m[:, :, 0:1], 0.5, None, ALU.mult)
            nc.vector.scalar_tensor_tensor(half_diff, half_diff, 0.25, half_diff, ALU.mult, ALU.mult)
            nc.vector.tensor_scalar(m[:, :, 1:2], m[:, :, 1:2], 1.0 / D, EPS, ALU.mult, ALU.add)
            dve.drain()
            nc.vector.tensor_tensor(m[:, :, 2:3], m[:, :, 1:2], half_diff, ALU.add).then_inc(moments_set, 1)
            dve.wait_ge(rooted, 1)
            nc.vector.reciprocal(core.moments[:, :, 2:3], core.moments[:, :, 1:2])

        @block.scalar
        def _(act):
            act.wait_ge(moments_set, 1)
            nc.scalar.activation(core.moments[:, :, 1:2], core.moments[:, :, 2:3], ACT.Sqrt).then_inc(rooted, 1)


def normalized(nc, core, out, x, b):
    m = core.moments[:, bass.ds(b, 1)].rearrange("p o n -> p (o n)")
    return nc.vector.tensor_scalar(out, x, m[:, 0:1], m[:, 2:3], ALU.subtract, ALU.mult)


def cols(b, width, base=0, n=None):
    return bass.ds(b * width + base, n or width)


def gat1_tables(nc, core, x, w1, al1, ar1, table):
    xs = core.arena[:, 0:NB * D]
    wk = core.hot[:, 0:2, 0:D + 2 * H1]
    rows = core.work[:, 8 * D:8 * D + 2 * ROW1].rearrange("p (r n) -> p r n", r=2)
    add_attention_columns(nc, core, w1, (al1, ar1), H1, wk, x, xs)

    row_moments(nc, core, "x0", (), lambda s: xs[:, cols(s, D)])

    def prepare(dve, s, tile, r, _):
        return normalized(nc, core, tile, xs[:, cols(s, D)], s)

    def finish(dve, s, prod, r):
        head = rows[:, r, 0:D + H1].rearrange("p (h c) -> p h c", h=H1)
        nc.vector.tensor_copy(head[:, :, 0:HD], prod[:, 0:D].rearrange("p (h c) -> p h c", h=H1))
        nc.vector.tensor_copy(rows[:, r, D + H1:ROW1], prod[:, D:D + H1])
        nc.vector.tensor_copy(core.el[:, :, bass.ds(s, 1)], prod[:, D:D + H1].unsqueeze(2))
        return nc.vector.tensor_copy(core.er[:, :, bass.ds(s, 1)], prod[:, D + H1:D + 2 * H1].unsqueeze(2))

    def store(sp, s, r):
        return sp.dma_start(table[bass.ds(s * P, P), :], rows[:, r])

    with nc.Block() as block:
        @block.vector
        def _(dve):
            nc.vector.memset(rows, 1.0)
    dense_tiles(nc, "g1", core, [wk[:, 0], wk[:, 1]], D + 2 * H1, None, prepare, finish, store)


def add_attention_columns(nc, core, w, vecs, heads, wk, x=None, xs=None):
    hd = D // heads
    a = core.work[:, 0:2 * D].rearrange("p (v n) -> p v n", v=2)
    prod = core.work[:, 2 * D:4 * D]
    with ExitStack() as st:
        w_in, x_in, zeroed = sems(nc, st, "w_in x_in tail_zeroed")
        block = st.enter_context(nc.Block())

        @block.sync
        def _(sp):
            sp.dma_start(wk[:, :, 0:D], w.rearrange("(k p) n -> p k n", p=P)).then_inc(w_in, 16)
            for v in range(2):
                sp.dma_start(a[:, v], vecs[v].rearrange("h d -> (h d)").partition_broadcast(P)).then_inc(w_in, 16)
            if x is not None:
                full = xs.rearrange("p (b n) -> p b n", b=NB)
                sp.dma_start(full[:, 0:NB - 1], x[0:(NB - 1) * P, :].rearrange("(b p) n -> p b n", p=P)).then_inc(x_in, 16)
                sp.wait_ge(zeroed, 1)
                sp.dma_start(full[0:TAIL, NB - 1], x[(NB - 1) * P:N, :]).then_inc(x_in, 16)
                sp.wait_ge(x_in, 32)

        @block.vector
        def _(dve):
            if x is not None:
                nc.vector.memset(xs[:, (NB - 1) * D:NB * D], 0.0).then_inc(zeroed, 1)
            dve.wait_ge(w_in, 48)
            for k in range(2):
                for v in range(2):
                    dve.drain()
                    nc.vector.tensor_tensor(prod[:, 0:D], wk[:, k, 0:D], a[:, v], ALU.mult)
                    dve.drain()
                    nc.vector.tensor_reduce(wk[:, k, D + v * heads:D + (v + 1) * heads],
                                            prod[:, 0:D].rearrange("p (h d) -> p h d", h=heads), AX.X, ALU.add)


def spread_attention(nc, core, heads):
    sb = core.work
    turned = sb[0:NB, 0:heads * P].rearrange("b (h p) -> b h p", h=heads)
    small = sb[:, 1024:1024 + 256]
    with ExitStack() as st:
        min_set, min_turned, min_all, min_spread, er_turned, er_copied, er_spread, er_used = sems(
            nc, st, "min_set min_turned min_all min_spread er_turned er_copied er_spread er_used")
        block = st.enter_context(nc.Block())

        @block.vector
        def _(dve):
            nc.vector.tensor_reduce(small[:, 0:1], core.el[:, 0:heads], AX.XY, ALU.min).then_inc(min_set, 1)
            dve.wait_ge(min_turned, 1)
            nc.vector.tensor_reduce(small[0:1, 1:2], core.bank(0, P)[0:1, :], AX.X, ALU.min).then_inc(min_all, 1)
            dve.wait_ge(min_spread, 1)
            nc.vector.tensor_scalar(core.low[:, 0:1], core.bank(1, 1), -1.0, None, ALU.add)
            nc.vector.tensor_scalar(core.low[:, 1:2], core.bank(1, 1), -1.0, 1.0, ALU.mult, ALU.add)
            dve.wait_ge(er_turned, heads)
            for h in range(heads):
                last = nc.vector.tensor_copy(turned[:, h], core.bank(2, heads * P)[0:NB, h * P:(h + 1) * P])
            last.then_inc(er_copied, 1)
            er, parts = core.er_steps, core.er_parts
            for h in range(heads):
                dve.wait_ge(er_spread, h + 1)
                nc.vector.tensor_copy(core.er_steps[:, h].rearrange("p (a k) -> p a k", a=2),
                                      core.psum[:, 2048 + h * 1024:3072 + h * 1024]
                                      .rearrange("p (a k) -> p a k", a=2)[:, :, 0:SK // 2])
            rest = core.work[:, 2048:2048 + heads * SK].rearrange("p (h k) -> p h k", h=heads)
            dve.drain()
            nc.vector.tensor_copy(parts[:, 0, 0:heads], er[:, 0:heads])
            dve.drain()
            nc.vector.tensor_tensor(rest, er[:, 0:heads], parts[:, 0, 0:heads], ALU.subtract)
            dve.drain()
            nc.vector.tensor_copy(parts[:, 1, 0:heads], rest)
            dve.drain()
            nc.vector.tensor_tensor(parts[:, 2, 0:heads], rest, parts[:, 1, 0:heads], ALU.subtract)

        @block.tensor
        def _(pe):
            pe.wait_ge(min_set, 1)
            nc.tensor.transpose(core.bank(0, P)[0:1, :], small[:, 0:1], core.ident[:]).then_inc(min_turned, 1)
            for h in range(heads):
                nc.tensor.transpose(core.bank(2, heads * P)[0:NB, h * P:(h + 1) * P], core.er[:, h], core.ident[:])\
                    .then_inc(er_turned, 1)
            pe.wait_ge(min_all, 1)
            nc.tensor.matmul(core.bank(1, 1), core.ones[0:1, :], small[0:1, 1:2], start=True, stop=True).then_inc(min_spread, 1)
            pe.wait_ge(er_copied, 1)
            for h in range(heads):
                for a in range(2):
                    last = nc.tensor.matmul(core.bank(4 + 2 * h + a, SK // 2), turned[:, h],
                                            core.step_sel[:, a * (SK // 2):(a + 1) * (SK // 2)], start=True, stop=True)
                last.then_inc(er_spread, 1)


def edge_pass(nc, core, name, table, row, heads, attend):
    G4 = GS * heads
    unit = row // heads if not attend else (D // heads + 1)
    el0 = heads * unit
    ring = core.work[:, 0:RING * GS * row].rearrange("p (r j n) -> p r j n", r=RING, j=GS)
    low = 0

    def take(n):
        nonlocal low
        low += n
        return core.arena[:, low - n:low]

    if attend:
        masked = take(G4 * P).rearrange("p (j h d) -> p j h d", j=GS, h=heads)
        weighted = take(2 * GS * heads * unit).rearrange("p (r j n) -> p r j n", r=2, j=GS)
        pick_t = take(GS * P).bitcast(BF16).rearrange("p (r j e) -> p r j e", r=2, j=GS)
        dl_ring = take(GS * P).bitcast(BF16).rearrange("p (r n) -> p r n", r=2)
        edge = take(11 * G4).rearrange("p (n j h) -> p n j h", n=11, j=GS)
        run_max = take(2 * heads * (GS + 1)).rearrange("p (r h j) -> p r h j", r=2, h=heads)
        kept_max = take(2 * heads * (GS + 1)).rearrange("p (r h j) -> p r h j", r=2, h=heads)
        known = take(6 * G4).bitcast(BF16).rearrange("p (r i j n) -> p r i j n", r=2, i=3, j=GS)
        scale = take(RING * G4).rearrange("p (r j h) -> p r j h", r=RING, j=GS)
        top, lifted, slope, drop_a, drop, lift, term, term_s, gap, gap_c, weight = (edge[:, n] for n in range(11))
        assert low <= AGG0
    pick = core.hot[:].rearrange("p r (j d) -> p r j d", j=GS)
    idx_ring = core.idx_ring
    turned = core.psum[:, 0:G4 * P]
    at_edge = core.bank(4, GS * 2 * heads).rearrange("p (j n) -> p j n", j=GS)

    sum_banks = (5, 6, 7) if heads == 2 else (2, 3, 5, 6)

    def sums(j):
        return core.bank(sum_banks[j % len(sum_banks)], heads * unit)

    def bank_back(j):
        back = 1
        while (j - back) % GS % len(sum_banks) != j % len(sum_banks):
            back += 1
        return back

    SLOTS = NG + 3
    with ExitStack() as st:
        names = ("idx_set pick_set terms_set masked_set turned_done top_read max_set edge_done gap_set "
                 "weight_set scale_set dl_free weighted_set lifted_set slope_set run_set part_set kept_set drop_set "
                 "fall_set term_set score_set edge_read").split()
        (idx_set, pick_set, terms_set, masked_set, turned_done, top_read, max_set, edge_done, gap_set,
         weight_set, scale_set, dl_free, weighted_set, lifted_set, slope_set, run_set, part_set, kept_set,
         drop_set, fall_set, term_set, score_set, edge_read) = sems(
            nc, st, " ".join(f"{name}_{x}" for x in names))
        rows_in = [core.stack.enter_context(nc.semaphore(f"{name}_rows_in{r}")) for r in range(RING)]
        sums_done = ring_sems(nc, st, f"{name}_sums_done", GS)
        added = ring_sems(nc, st, f"{name}_added", GS)
        dl_in = ring_sems(nc, st, f"{name}_dl_in", 2)
        block = st.enter_context(nc.Block())

        @block.gpsimd
        def _(pool):
            def slot(s, c, t):
                pool.wait_ge(idx_set, s + 1)
                if attend:
                    ge(pool, weighted_set, 2 * (s - RING + 1))
                else:
                    ge(pool, sums_done[GS - 1], s - RING + 1)
                pool.nop(nofuse=True)
                for j in range(GS):
                    nc.gpsimd.indirect_dma_start(
                        ring[:, c, j], None, table,
                        bass.IndirectOffsetOnAxis(ap=idx_ring[:, c, j:j + 1], axis=0)).then_inc(rows_in[c], 16)
            unrolled(pool, NG, RING, slot, 4, 2)

        if attend:
            @block.sync
            def _(sp):
                def slot(s, c, t):
                    ge(sp, dl_free, s - 1)
                    sp.dma_start(dl_ring[:, c % 2],
                                 core.dl_rows.rearrange("k e -> (k e)")[cols(s, GS * P)].partition_broadcast(P))\
                        .then_inc(dl_in[c % 2], 16)
                unrolled(sp, NG, RING, slot, 4, 2)

        @block.vector
        def _(dve):
            def select(g, q, t):
                ge(dve, sums_done[GS - 1], g - RING + 1)
                nc.vector.tensor_tensor(
                    pick[:, q], core.iota_col[:].unsqueeze(1).to_broadcast([P, GS, P]),
                    core.step_dst[:, cols(g, GS)].unsqueeze(2).to_broadcast([P, GS, P]), ALU.is_equal)\
                    .then_inc(pick_set, 1)

            def raise_terms(g, q, t):
                dve.wait_ge(rows_in[q], (t + 1) * 16 * GS)
                ge(dve, masked_set, 2 * g)
                nc.vector.tensor_scalar(lift, ring[:, q, :, el0:el0 + heads], core.low[:, 1:2], None, ALU.add)\
                    .then_inc(terms_set, 1)

            def slot(s, c, t):
                new, mid, old = in_range(s, 0, NG - 1), in_range(s, 1, NG + 1), in_range(s, 3, SLOTS)
                r = (c + 1) % 2
                gm, go = s - 1, s - 3
                if old:
                    if attend:
                        dve.wait_ge(scale_set, s - 2)
                    same = core.step_same[:, cols(go, GS)]
                    _, at = nc.values_load_multi_w_load_instructions(
                        core.step_at[0:1, cols(go, GS)], engines=[mybir.EngineType.DVE], min_val=AGG0,
                        max_val=ARENA - ACW,
                        skip_runtime_bounds_check_because="a step's block is a count of at most NB - 1 starts")

                def add(j):
                    if not old:
                        return
                    dve.wait_ge(sums_done[j], go + 1)
                    for h in range(heads):
                        ge(dve, added[(j - 1) % GS], (go if j else go - 1) * heads + h + 1)
                        own = core.arena[:, bass.ds(at[j] + h * unit, unit)]
                        keep = scale[:, (c - 3) % RING, j, h:h + 1] if attend else same[:, j:j + 1]
                        nc.vector.scalar_tensor_tensor(own, own, keep, sums(j)[:, h * unit:(h + 1) * unit],
                                                       ALU.mult, ALU.add).then_inc(added[j], 1)

                if not attend:
                    for j in range(GS):
                        add(j)
                    if new:
                        select(s + 1, (c + 1) % RING, turn(t, c, -1, RING))
                    return
                if mid:
                    dve.wait_ge(turned_done, s)
                    nc.vector.tensor_reduce(top.rearrange("p j h -> p (j h)"),
                                            turned.rearrange("p (n e) -> p n e", e=P), AX.X, ALU.max)\
                        .then_inc(top_read, 1)
                    ge(dve, edge_done, s - 2)
                    nc.vector.tensor_copy(known[:, r, :, :, 0:heads].rearrange("p i j h -> p i h j"),
                                          core.er_parts[:, :, 0:heads, cols(gm, GS)])
                    nc.vector.tensor_copy(kept_max[:, r, :, 0:1], kept_max[:, 1 - r, :, GS:GS + 1])
                    dve.wait_ge(top_read, s)
                    nc.vector.scalar_tensor_tensor(
                        lifted, top, core.low[:, 0:1], core.er_steps[:, 0:heads, cols(gm, GS)].rearrange("p h j -> p j h"),
                        ALU.add, ALU.add).then_inc(lifted_set, 1)
                if mid:
                    dve.wait_ge(lifted_set, s)
                    nc.vector.scalar_tensor_tensor(slope, lifted, SLOPE, lifted, ALU.mult, ALU.max)\
                        .then_inc(slope_set, 1)
                if in_range(s, 0, NG):
                    dve.wait_ge(dl_in[c % 2], (t * (RING // 2) + c // 2 + 1) * 16)
                    ge(dve, edge_done, s - 1)
                    nc.vector.tensor_scalar(pick_t[:, c % 2].rearrange("p j e -> p (j e)"), dl_ring[:, c % 2],
                                            core.part[:, 0:1], None, ALU.is_equal).then_inc(dl_free, 1)
                if mid:
                    reset = core.step_reset[:, cols(gm, GS)]
                    now = run_max[:, r, :, 1:GS + 1]
                    part = [known[:, r, i, :, heads:2 * heads].rearrange("p j h -> p h j") for i in range(2)]
                    dve.wait_ge(slope_set, s)
                    for h in range(heads):
                        nc.vector.tensor_tensor_scan(run_max[:, r, h, 1:GS + 1], reset, slope[:, :, h],
                                                     run_max[:, 1 - r, h, GS:GS + 1], ALU.add, ALU.max)\
                            .then_inc(run_set, 1)
                add(0)
                if mid:
                    dve.wait_ge(run_set, s * heads)
                    nc.vector.tensor_copy(part[0], now).then_inc(part_set, 1)
                if new:
                    raise_terms(s + 1, (c + 1) % RING, turn(t, c, -1, RING))
                if mid:
                    dve.wait_ge(part_set, s)
                    nc.vector.tensor_tensor(part[1], now, part[0], ALU.subtract).then_inc(max_set, 1)
                add(1)
                if mid:
                    dve.wait_ge(max_set, s)
                    nc.vector.tensor_tensor(kept_max[:, r, :, 1:GS + 1], part[0], part[1], ALU.add)\
                        .then_inc(kept_set, 1)
                add(2)
                if mid:
                    dve.wait_ge(kept_set, s)
                    nc.vector.tensor_tensor(drop_a.rearrange("p j h -> p h j"), kept_max[:, r, :, 0:GS],
                                            reset.unsqueeze(1).to_broadcast([P, heads, GS]), ALU.add)\
                        .then_inc(drop_set, 1)
                add(3)
                if mid:
                    dve.wait_ge(drop_set, s)
                    ge(dve, scale_set, s - 1)
                    nc.vector.tensor_tensor(drop.rearrange("p j h -> p h j"), drop_a.rearrange("p j h -> p h j"),
                                            kept_max[:, r, :, 1:GS + 1], ALU.subtract).then_inc(fall_set, 1)
                    dve.wait_ge(edge_done, s)
                    nc.vector.tensor_tensor(term, ring[:, (c - 1) % RING, :, el0:el0 + heads],
                                            at_edge[:, :, 0:heads], ALU.add).then_inc(term_set, 1)
                add(4)
                if mid:
                    dve.wait_ge(term_set, s)
                    nc.vector.scalar_tensor_tensor(term_s, term, SLOPE, term, ALU.mult, ALU.max)\
                        .then_inc(score_set, 1)
                add(5)
                if mid:
                    dve.wait_ge(score_set, s)
                    nc.vector.tensor_tensor(gap, term_s, at_edge[:, :, heads:2 * heads], ALU.subtract)\
                        .then_inc(edge_read, 1)
                add(6)
                if mid:
                    dve.wait_ge(edge_read, s)
                    ge(dve, weight_set, s - 1)
                    nc.vector.tensor_scalar(gap_c, gap, 30.0, None, ALU.min).then_inc(gap_set, 1)
                add(7)
                if new:
                    select(s + 1, (c + 1) % RING, turn(t, c, -1, RING))

            if attend:
                nc.vector.memset(run_max, 0.0)
                nc.vector.memset(kept_max, 0.0)
                nc.vector.memset(known, 0.0)
                dve.drain()
            select(0, 0, 0)
            if attend:
                raise_terms(0, 0, 0)
            unrolled(dve, SLOTS, RING, slot, 4, 4)

        @block.tensor
        def _(pe):
            def slot(s, c, t):
                mid, old = in_range(s, 1, NG + 1), in_range(s, 3, SLOTS)
                go = s - 3

                def sum_step(j):
                    back = j - bank_back(j)
                    ge(pe, added[back % GS], (go + 1 if back >= 0 else go) * heads)
                    rhs = weighted[:, (c - 3) % 2, j] if attend else ring[:, (c - 3) % RING, j, 0:unit]
                    nc.tensor.matmul(sums(j), pick[:, (c - 3) % RING, j], rhs, start=True, stop=True)\
                        .then_inc(sums_done[j], 1)

                if not attend:
                    if old:
                        pe.wait_ge(pick_set, s - 2)
                        pe.wait_ge(rows_in[(c - 3) % RING], (turn(t, c, 3, RING) + 1) * 16 * GS)
                        for j in range(GS):
                            sum_step(j)
                    return
                if old:
                    pe.wait_ge(weighted_set, 2 * go + 1)
                    for j in range(2):
                        sum_step(j)
                if mid:
                    pe.wait_ge(max_set, s)
                    pe.wait_ge(dl_free, s)
                    ge(pe, edge_read, s - 1)
                    for j in range(GS):
                        for i in range(3):
                            last = nc.tensor.matmul(at_edge[:, j], pick_t[:, (c + 1) % 2, j],
                                                    known[:, (c + 1) % 2, i, j], start=(i == 0), stop=(i == 2))
                    last.then_inc(edge_done, 1)
                if old:
                    for j in range(2, GS):
                        if j == 4:
                            pe.wait_ge(weighted_set, 2 * go + 2)
                        sum_step(j)
                if in_range(s, 0, NG):
                    ge(pe, top_read, s)
                    for j in range(GS):
                        if j % 4 == 0:
                            pe.wait_ge(masked_set, 2 * s + j // 4 + 1)
                        for h in range(heads):
                            n = j * heads + h
                            last = nc.tensor.transpose(turned[:, n * P:(n + 1) * P], masked[:, j, h], core.ident[:])
                    last.then_inc(turned_done, 1)
            unrolled(pe, SLOTS, RING, slot, 4, 4)

        @block.scalar
        def _(act):
            def stage(g, q):
                nc.scalar.copy(idx_ring[:, q], core.step_idx[:, cols(g, GS)]).then_inc(idx_set, 1)

            def slot(s, c, t):
                if in_range(s, 0, NG - 2):
                    ge(act, rows_in[(c + 3) % RING], turn(t, c, -3, RING) * 16 * GS)
                    stage(s + 3, (c + 3) % RING)
                if not attend:
                    return
                if in_range(s, 0, NG):
                    act.wait_ge(pick_set, s + 1)
                    act.wait_ge(terms_set, s + 1)
                    ge(act, turned_done, s)
                    for j in range(GS):
                        for h in range(heads):
                            last = nc.scalar.activation(masked[:, j, h], pick[:, c, j], ACT.Copy,
                                                        scale=lift[:, j, h:h + 1])
                        if j % 4 == 3:
                            last.then_inc(masked_set, 1)
                if in_range(s, 2, NG + 2):
                    go, r = s - 2, c % 2
                    act.wait_ge(gap_set, s - 1)
                    ge(act, weighted_set, 2 * go)
                    nc.scalar.activation(weight, gap_c, ACT.Exp).then_inc(weight_set, 1)
                    act.wait_ge(weight_set, s - 1)
                    ge(act, sums_done[GS - 1], go - 1)
                    for j in range(GS):
                        for h in range(heads):
                            last = nc.scalar.activation(weighted[:, r, j, h * unit:(h + 1) * unit],
                                                        ring[:, (c - 2) % RING, j, h * unit:(h + 1) * unit],
                                                        ACT.Copy, scale=weight[:, j, h:h + 1])
                        if j % 4 == 3:
                            last.then_inc(weighted_set, 1)
                if in_range(s, 1, NG + 1):
                    act.wait_ge(fall_set, s)
                    ge(act, added[GS - 1], (s - RING) * heads)
                    nc.scalar.activation(scale[:, (c - 1) % RING], drop, ACT.Exp).then_inc(scale_set, 1)
            for g in range(3):
                stage(g, g)
            unrolled(act, SLOTS if attend else NG, RING, slot, 4, 4)


def gat2_tables(nc, core, w2, al2, ar2, b1, table):
    wk = core.hot[:, 0:2, 0:D + 2]
    bias = core.hot[:, 2, 0:D]
    inv = core.hot[:, 3, 0:NB * H1].rearrange("p (b h) -> p b h", b=NB)
    rows = core.work[:, 8 * D:8 * D + 2 * ROW2].rearrange("p (r n) -> p r n", r=2)
    add_attention_columns(nc, core, w2, (al2, ar2), 1, wk)
    weight_sums(nc, core, "s1", H1, inv, b1, bias, rows)

    def prepare(dve, s, tile, r, _):
        for h in range(H1):
            last = nc.vector.scalar_tensor_tensor(
                tile[:, h * HD:(h + 1) * HD], core.arena[:, cols(s, ACW, AGG0 + h * (HD + 1), HD)],
                inv[:, bass.ds(s, 1), h:h + 1].rearrange("p o n -> p (o n)"), bias[:, h * HD:(h + 1) * HD],
                ALU.mult, ALU.add)
        return last

    def finish(dve, s, prod, r):
        nc.vector.tensor_copy(rows[:, r, 0:D], prod[:, 0:D])
        nc.vector.tensor_copy(rows[:, r, D + 1:ROW2], prod[:, D:D + 1])
        nc.vector.tensor_copy(core.el[:, 0:1, bass.ds(s, 1)], prod[:, D:D + 1].unsqueeze(2))
        return nc.vector.tensor_copy(core.er[:, 0:1, bass.ds(s, 1)], prod[:, D + 1:D + 2].unsqueeze(2))

    def store(sp, s, r):
        return sp.dma_start(table[bass.ds(s * P, P), :], rows[:, r])

    dense_tiles(nc, "g2", core, [wk[:, 0], wk[:, 1]], D + 2, None, prepare, finish, store, func=ACT.Relu)


def weight_sums(nc, core, name, heads, inv, vec, bias, rows=None):
    unit = D // heads
    agg = core.arena[:, AGG0:ARENA].rearrange("p (b n) -> p b n", b=NB)
    sums = agg[:, :, 0:heads * (unit + 1)].rearrange("p b (h c) -> p b h c", h=heads)[:, :, :, unit]
    with ExitStack() as st:
        vec_in, = sems(nc, st, f"{name}_vec_in")
        block = st.enter_context(nc.Block())

        @block.sync
        def _(sp):
            sp.dma_start(bias, vec.rearrange("h d -> (h d)").partition_broadcast(P)).then_inc(vec_in, 16)
            sp.wait_ge(vec_in, 16)

        @block.vector
        def _(dve):
            if rows is not None:
                nc.vector.memset(rows, 1.0)
            nc.vector.tensor_scalar(inv, sums, 1.0e-30, None, ALU.max)
            dve.drain()
            nc.vector.reciprocal(inv, inv)


def block_chunks(rows, view, last_rows):
    step = NB // 7
    for q in range(7):
        lo, hi = q * step, (q + 1) * step
        full = min(hi, NB - 1) if last_rows < P else hi
        yield view[:, lo:full], rows[lo * P:full * P, :].rearrange("(b p) n -> p b n", p=P)
        if hi > full:
            yield view[0:last_rows, full], rows[full * P:full * P + last_rows, :]


def first_residual(nc, core, x, b2, x1_rows):
    inv = core.hot[:, 3, 0:NB].rearrange("p (b h) -> p b h", b=NB)
    bias = core.hot[:, 2, 0:D]
    xs = core.arena[:, 0:NB * D]
    full = xs.rearrange("p (b n) -> p b n", b=NB)
    weight_sums(nc, core, "s2", 1, inv, b2, bias)
    agg = core.arena[:, AGG0:ARENA].rearrange("p (b n) -> p b n", b=NB)[:, :, 0:D]
    with ExitStack() as st:
        tail_zeroed, = sems(nc, st, "x_tail_zeroed")
        x_in = ring_sems(nc, st, "x_in", 8)
        block = st.enter_context(nc.Block())

        @block.sync
        def _(sp):
            for q, (part, rows) in enumerate(block_chunks(x, full, TAIL)):
                if q == 7:
                    sp.wait_ge(tail_zeroed, 1)
                sp.dma_start(part, rows).then_inc(x_in[q], 16)
            for q in range(8):
                sp.wait_ge(x_in[q], 16)

        @block.vector
        def _(dve):
            nc.vector.memset(full[:, NB - 1], 0.0).then_inc(tail_zeroed, 1)

    def place(s):
        return core.arena[:, cols(s, ACW, AGG0, D)]

    def own_part(dve, s, r):
        nc.vector.scalar_tensor_tensor(place(s), place(s), inv[:, bass.ds(s, 1), 0:1].rearrange("p o n -> p (o n)"),
                                       xs[:, cols(s, D)], ALU.mult, ALU.add)

    def add_bias(dve, s, r):
        nc.vector.tensor_tensor(place(s), place(s), bias, ALU.add)

    row_moments(nc, core, "x1", (own_part, add_bias), place)
    with ExitStack() as st:
        kept, = sems(nc, st, "x1_kept")
        block = st.enter_context(nc.Block())

        @block.sync
        def _(sp):
            for n, (part, rows) in enumerate(block_chunks(x1_rows, agg, P)):
                sp.dma_start(rows, part).then_inc(kept, 16)
            sp.wait_ge(kept, 16 * 7)


def slice_logits(nc, core, w_xt, b_x, w_slice, b_slice, temp, wl, bl):
    HC = NH * NSL
    wx = core.work[0:DH, 0:NH * D].rearrange("c (h k) -> c h k", h=NH)
    ws = core.work[0:DH, 2048:2048 + NSL]
    bx = core.work[0:DH, 2112:2112 + NH]
    bx_wide = core.work[0:DH, 2120:2120 + NH * P].rearrange("c (h p) -> c h p", h=NH)
    bs = core.work[:, 3200:3200 + NSL]
    inv_t = core.work[:, 3264:3264 + NH]
    biased = core.work[:, 3300:3300 + HC].rearrange("p (h g) -> p h g", h=NH)
    with ExitStack() as st:
        weights_in, bias_wide_set, maps_done = sems(nc, st, "weights_in bias_wide_set maps_done")
        block = st.enter_context(nc.Block())

        @block.sync
        def _(sp):
            for t, a in ((wx, w_xt.rearrange("(h c) k -> c h k", h=NH)), (ws, w_slice),
                         (bx, b_x), (bs, b_slice.partition_broadcast(P)),
                         (inv_t, temp.partition_broadcast(P))):
                sp.dma_start(t, a).then_inc(weights_in, 16)

        @block.tensor
        def _(pe):
            pe.wait_ge(weights_in, 80)
            for k in range(2):
                for h in range(NH):
                    nc.tensor.matmul(core.bank(k)[:, h * NSL:(h + 1) * NSL], wx[:, h, k * P:(k + 1) * P], ws,
                                     start=True, stop=True)
            pe.wait_ge(bias_wide_set, 1)
            for h in range(NH):
                last = nc.tensor.matmul(core.bank(2)[:, h * NSL:(h + 1) * NSL], bx_wide[:, h], ws, start=True, stop=True)
            last.then_inc(maps_done, 1)

        @block.vector
        def _(dve):
            dve.wait_ge(weights_in, 80)
            nc.vector.tensor_copy(bx_wide, bx.unsqueeze(2).to_broadcast([DH, NH, P])).then_inc(bias_wide_set, 1)
            nc.vector.tensor_scalar(inv_t, inv_t, 0.1, 5.0, ALU.max, ALU.min)
            dve.drain()
            nc.vector.reciprocal(inv_t, inv_t)
            dve.drain()
            dve.wait_ge(maps_done, 1)
            wide = inv_t.unsqueeze(2).to_broadcast([P, NH, NSL])
            for k in range(2):
                nc.vector.tensor_tensor(wl[:, k].rearrange("p (h g) -> p h g", h=NH),
                                        core.bank(k).rearrange("p (h g) -> p h g", h=NH), wide, ALU.mult)
            nc.vector.tensor_tensor(biased, core.bank(2).rearrange("p (h g) -> p h g", h=NH),
                                    bs.unsqueeze(1).to_broadcast([P, NH, NSL]), ALU.add)
            dve.drain()
            nc.vector.tensor_tensor(bl.rearrange("p (h g) -> p h g", h=NH), biased, wide, ALU.mult)


def slice_weights(nc, core, wl, bl):
    HC = NH * NSL
    xl = core.work[:, 0:4 * D].rearrange("p (r n) -> p r n", r=4)
    xlt = core.work[:, 4 * D:6 * D].rearrange("p (r n) -> p r n", r=2)
    logits = core.work[:, 1536:1536 + 2 * HC].rearrange("p (r n) -> p r n", r=2)
    expd = core.work[:, 2560:2560 + 2 * HC].rearrange("p (r n) -> p r n", r=2)
    sw = core.work[:, 3584:3584 + 2 * HC].rearrange("p (r n) -> p r n", r=2)
    total = core.work[:, 4608:4608 + HC]
    high, weight_sum, inv = (core.work[:, 5120 + 8 * n:5128 + 8 * n] for n in range(3))

    def by_head(t):
        return t.rearrange("p (h g) -> p h g", h=NH)

    def wide(t):
        return t.unsqueeze(2).to_broadcast([P, NH, NSL])

    SLOTS = NB + 3
    with ExitStack() as st:
        (tile_set, tile_turned, tile_copied, product, biased, shifted, exp_set, sw_set, sw_turned, swt_copied,
         tokens_done, totalled) = sems(nc, st, "tile_set tile_turned tile_copied product biased shifted exp_set sw_set "
                                               "sw_turned swt_copied tokens_done totalled")
        block = st.enter_context(nc.Block())

        @block.vector
        def _(dve):
            def slot(s, c, t):
                new, mid, old = in_range(s, 0, NB), in_range(s, 1, NB + 1), in_range(s, 2, NB + 2)
                m, o = (c + 1) % 2, c % 2
                if new:
                    ge(dve, tokens_done, s - 3)
                    normalized(nc, core, xl[:, c], core.arena[:, cols(s, ACW, AGG0, D)], s).then_inc(tile_set, 1)
                if mid:
                    dve.wait_ge(product, s)
                    nc.vector.tensor_tensor(logits[:, m], core.bank(2 + m), bl, ALU.add).then_inc(biased, 1)
                if old:
                    dve.wait_ge(exp_set, s - 1)
                    nc.vector.tensor_reduce(weight_sum, by_head(expd[:, o]), AX.X, ALU.add)
                dve.drain()
                if mid:
                    nc.vector.tensor_reduce(high, by_head(logits[:, m]), AX.X, ALU.max)
                if old:
                    nc.vector.reciprocal(inv, weight_sum)
                dve.drain()
                if mid:
                    nc.vector.tensor_tensor(by_head(expd[:, m]), by_head(logits[:, m]), wide(high), ALU.subtract)\
                        .then_inc(shifted, 1)
                if old:
                    ge(dve, tokens_done, s - 3)
                    ge(dve, totalled, s - 2)
                    nc.vector.tensor_tensor(by_head(sw[:, o]), by_head(expd[:, o]), wide(inv), ALU.mult)\
                        .then_inc(sw_set, 1)
            unrolled(dve, NB + 2, 4, slot, 4, 4)

        @block.scalar
        def _(act):
            def slot(s, c, t):
                if in_range(s, 0, NB):
                    act.wait_ge(tile_turned, s + 1)
                    ge(act, product, s - 1)
                    nc.scalar.activation(xlt[:, c % 2], core.bank(c % 2, D), ACT.Copy).then_inc(tile_copied, 1)
                if in_range(s, 1, NB + 1):
                    act.wait_ge(shifted, s)
                    nc.scalar.activation(expd[:, (c + 1) % 2], expd[:, (c + 1) % 2], ACT.Exp).then_inc(exp_set, 1)
                if in_range(s, 3, SLOTS):
                    act.wait_ge(sw_turned, s - 2)
                    nc.scalar.activation(core.arena[:, cols(s - 3, HC)], core.bank(6 + (c + 1) % 2), ACT.Copy)\
                        .then_inc(swt_copied, 1)
            unrolled(act, SLOTS, 4, slot, 4, 4)

        @block.gpsimd
        def _(pool):
            nc.gpsimd.memset(total, 0.0).then_inc(totalled, 1)

            def slot(s, c, t):
                pool.wait_ge(totalled, s + 1)
                pool.wait_ge(sw_set, s + 1)
                rows = TAIL if isinstance(s, int) and s == NB - 1 else P
                nc.gpsimd.tensor_tensor(total[0:rows], total[0:rows], sw[0:rows, c % 2], ALU.add).then_inc(totalled, 1)
            unrolled(pool, NB, 2, slot, 2, 2)

        @block.tensor
        def _(pe):
            def slot(s, c, t):
                if in_range(s, 0, NB):
                    pe.wait_ge(tile_set, s + 1)
                    ge(pe, tile_copied, s - 1)
                    for k in range(2):
                        last = nc.tensor.transpose(core.bank(c % 2)[:, k * P:(k + 1) * P], xl[:, c, k * P:(k + 1) * P],
                                                   core.ident[:])
                    last.then_inc(tile_turned, 1)
                if in_range(s, 3, SLOTS):
                    r = (c + 1) % 2
                    rows = TAIL if isinstance(s, int) and s == SLOTS - 1 else P
                    pe.wait_ge(sw_set, s - 2)
                    ge(pe, swt_copied, s - 4)
                    for q in range(4):
                        last = nc.tensor.transpose(core.bank(6 + r)[:, q * P:(q + 1) * P], sw[:, r, q * P:(q + 1) * P],
                                                   core.ident[:])
                    last.then_inc(sw_turned, 1)
                    for k in range(2):
                        last = nc.tensor.matmul(core.bank(4 + k), xl[0:rows, (c + 1) % 4, k * P:(k + 1) * P],
                                                sw[0:rows, r], start=isinstance(s, int) and s == 3,
                                                stop=isinstance(s, int) and s == SLOTS - 1)
                    last.then_inc(tokens_done, 1)
                if in_range(s, 1, NB + 1):
                    pe.wait_ge(tile_copied, s)
                    ge(pe, biased, s - 2)
                    for k in range(2):
                        last = nc.tensor.matmul(core.bank(2 + (c + 1) % 2), xlt[:, (c + 1) % 2, k * P:(k + 1) * P],
                                                wl[:, k], start=(k == 0), stop=(k == 1))
                    last.then_inc(product, 1)
            unrolled(pe, SLOTS, 4, slot, 4, 4)
    return total


def slice_attention(nc, core, total, w_fx, b_fx, w_q, w_k, w_v, w_out, v2):
    HC = NH * NSL
    at = [0]

    def scratch(n, parts=P):
        at[0] += n
        return core.work[0:parts, at[0] - n:at[0]]

    fx = scratch(2 * INNER).rearrange("p (k n) -> p k n", k=2)
    out_w = scratch(NH * D, DH).rearrange("c (h n) -> c h n", h=NH)
    sums = scratch(2 * HC).rearrange("p (k n) -> p k n", k=2)
    at[0] += HC
    assert at[0] == 4608
    at[0] += HC
    norm, inv_norm = scratch(HC, DH), scratch(HC, DH)
    token, qt, kt, v = (scratch(HC, DH) for _ in range(4))
    attn, attn_t, out_t = (scratch(HC, DH) for _ in range(3)) if at[0] + 3 * HC <= 8320 else (None,) * 3
    if attn is None:
        attn, attn_t, out_t = (core.hot[0:DH, 3, 0:HC], core.hot[0:DH, 3, HC:2 * HC], core.hot[0:DH, 2, 0:HC])
    qkv = core.hot[0:DH, 2, HC:HC + 3 * DH].rearrange("p (i n) -> p i n", i=3)
    bfx = core.hot[0:DH, 2, 800:800 + NH]
    high, weight_sum, inv = (core.hot[0:DH, 2, 808 + 8 * n:816 + 8 * n] for n in range(3))

    def by_head(t):
        return t.rearrange("p (h g) -> p h g", h=NH)

    def wide(t):
        return t.unsqueeze(2).to_broadcast([DH, NH, NSL])

    def head(t, h):
        return t[:, h * NSL:(h + 1) * NSL]

    with ExitStack() as st:
        (loaded, norm_done, sums_copied, maps_done, token_set, qkv_done, qkv_copied, scores_done, shifted, exp_set,
         attn_set, attn_turned, attn_copied, out_done, out_copied, v2_done) = sems(
            nc, st, "sl_loaded norm_done sums_copied maps_done token_set qkv_done qkv_copied scores_done sl_shifted "
                    "sl_exp_set attn_set attn_turned attn_copied out_done out_copied v2_done")
        block = st.enter_context(nc.Block())

        @block.sync
        def _(sp):
            for t, a in ((fx, w_fx.rearrange("(k p) n -> p k n", p=P)), (bfx, b_fx), (qkv[:, 0], w_q), (qkv[:, 1], w_k),
                         (qkv[:, 2], w_v), (out_w, w_out.rearrange("(h c) n -> c h n", h=NH))):
                sp.dma_start(t, a).then_inc(loaded, 16)

        @block.tensor
        def _(pe):
            nc.tensor.matmul(core.bank(0)[0:DH, :], core.ones[:, 0:DH], total, start=True, stop=True).then_inc(norm_done, 1)
            pe.wait_ge(loaded, 96)
            pe.wait_ge(sums_copied, 1)
            for h in range(NH):
                for k in range(2):
                    last = nc.tensor.matmul(head(core.bank(1)[0:DH], h), head(fx[:, k], h), head(sums[:, k], h),
                                            start=(k == 0), stop=(k == 1))
            last.then_inc(maps_done, 1)
            pe.wait_ge(token_set, 1)
            nc.tensor.matmul(core.bank(2)[0:DH], qkv[:, 0], token, start=True, stop=True)
            nc.tensor.matmul(core.bank(3)[0:DH], qkv[:, 1], token, start=True, stop=True)
            for h in range(NH):
                last = nc.tensor.matmul(head(core.bank(4)[0:DH], h), head(token, h), qkv[:, 2], start=True, stop=True)
            last.then_inc(qkv_done, 1)
            pe.wait_ge(qkv_copied, 1)
            for h in range(NH):
                last = nc.tensor.matmul(head(core.bank(5)[0:DH], h), head(qt, h), head(kt, h), start=True, stop=True)
            last.then_inc(scores_done, 1)
            pe.wait_ge(attn_set, 1)
            for h in range(NH):
                last = nc.tensor.transpose(head(core.bank(6)[0:DH], h), head(attn, h), core.ident[0:DH, 0:DH])
            last.then_inc(attn_turned, 1)
            pe.wait_ge(attn_copied, 1)
            for h in range(NH):
                last = nc.tensor.matmul(head(core.bank(7)[0:DH], h), head(v, h), head(attn_t, h), start=True, stop=True)
            last.then_inc(out_done, 1)
            pe.wait_ge(out_copied, 1)
            for j in range(NH // 2):
                for i in range(2):
                    last = nc.tensor.matmul(core.bank(j)[:, i * D:(i + 1) * D], out_t[:, j * P:(j + 1) * P],
                                            out_w[:, 2 * j + i], start=True, stop=True)
            last.then_inc(v2_done, 1)

        @block.vector
        def _(dve):
            for k in range(2):
                last = nc.vector.tensor_copy(sums[:, k], core.bank(4 + k))
            last.then_inc(sums_copied, 1)
            dve.wait_ge(norm_done, 1)
            nc.vector.tensor_copy(norm, core.bank(0)[0:DH])
            nc.vector.tensor_scalar(inv_norm, core.bank(0)[0:DH], EPS, None, ALU.add)
            dve.wait_ge(loaded, 96)
            dve.drain()
            nc.vector.reciprocal(inv_norm, inv_norm)
            nc.vector.tensor_tensor(by_head(norm), by_head(norm), wide(bfx), ALU.mult)
            dve.drain()
            dve.wait_ge(maps_done, 1)
            nc.vector.tensor_tensor(norm, norm, core.bank(1)[0:DH], ALU.add)
            dve.drain()
            nc.vector.tensor_tensor(token, norm, inv_norm, ALU.mult).then_inc(token_set, 1)
            dve.wait_ge(qkv_done, 1)
            for i, t in enumerate((qt, kt, v)):
                last = nc.vector.tensor_copy(t, core.bank(2 + i)[0:DH])
            last.then_inc(qkv_copied, 1)
            dve.wait_ge(scores_done, 1)
            nc.vector.tensor_reduce(high, by_head(core.bank(5)[0:DH]), AX.X, ALU.max)
            dve.drain()
            nc.vector.tensor_tensor(by_head(attn), by_head(core.bank(5)[0:DH]), wide(high), ALU.subtract).then_inc(shifted, 1)
            dve.wait_ge(exp_set, 1)
            nc.vector.tensor_reduce(weight_sum, by_head(attn), AX.X, ALU.add)
            dve.drain()
            nc.vector.reciprocal(inv, weight_sum)
            dve.drain()
            nc.vector.tensor_tensor(by_head(attn), by_head(attn), wide(inv), ALU.mult).then_inc(attn_set, 1)
            dve.wait_ge(attn_turned, 1)
            nc.vector.tensor_copy(attn_t, core.bank(6)[0:DH]).then_inc(attn_copied, 1)
            dve.wait_ge(out_done, 1)
            nc.vector.tensor_copy(out_t, core.bank(7)[0:DH]).then_inc(out_copied, 1)
            dve.wait_ge(v2_done, 1)
            for j in range(NH // 2):
                for i in range(2):
                    nc.vector.tensor_copy(v2[i * DH:(i + 1) * DH, j], core.bank(j)[i * DH:(i + 1) * DH, i * D:(i + 1) * D])

        @block.scalar
        def _(act):
            act.wait_ge(shifted, 1)
            nc.scalar.activation(attn, attn, ACT.Exp, scale=float(DH) ** -0.5).then_inc(exp_set, 1)


def second_residual(nc, core, v2, b_out, x1_rows, x2_rows):
    HC = NH * NSL
    bias = core.hot[:, 2, 0:D]
    x_ring = core.work[:, 0:4 * D].rearrange("p (r n) -> p r n", r=4)
    part_ring = core.work[:, 4 * D:8 * D].rearrange("p (r n) -> p r n", r=4)
    swt = core.work[:, 8 * D:8 * D + 2 * HC].rearrange("p (r q n) -> p r q n", r=2, q=4)
    with ExitStack() as st:
        bias_in, swt_copied, product, biased, x2_set, = sems(nc, st, "bias_in swt2_copied product2 biased2 x2_set")
        x_in = ring_sems(nc, st, "x1_in", 4)
        block = st.enter_context(nc.Block())

        @block.sync
        def _(sp):
            sp.dma_start(bias, b_out.partition_broadcast(P)).then_inc(bias_in, 16)

            def slot(s, c, t):
                ge(sp, x2_set, s - 3)
                sp.dma_start(x_ring[:, c], x1_rows[bass.ds(s * P, P), :]).then_inc(x_in[c], 16)
            unrolled(sp, NB, 4, slot, 4, 4)

        @block.scalar
        def _(act):
            def slot(s, c, t):
                ge(act, product, s - 1)
                nc.scalar.activation(swt[:, c % 2].rearrange("p q n -> p (q n)"), core.arena[:, cols(s, HC)], ACT.Copy)\
                    .then_inc(swt_copied, 1)
            unrolled(act, NB, 2, slot, 2, 2)

        @block.tensor
        def _(pe):
            def slot(s, c, t):
                pe.wait_ge(swt_copied, s + 1)
                ge(pe, biased, s - 1)
                for q in range(4):
                    last = nc.tensor.matmul(core.bank(c % 2, D), swt[:, c % 2, q], v2[:, q], start=(q == 0), stop=(q == 3))
                last.then_inc(product, 1)
            unrolled(pe, NB, 2, slot, 2, 2)

        @block.vector
        def _(dve):
            dve.wait_ge(bias_in, 16)

            def slot(s, c, t):
                if in_range(s, 0, NB):
                    dve.wait_ge(product, s + 1)
                    ge(dve, x2_set, s - 3)
                    nc.vector.tensor_tensor(part_ring[:, c], core.bank(c % 2, D), bias, ALU.add).then_inc(biased, 1)
                if in_range(s, 1, NB + 1):
                    dve.wait_ge(x_in[(c - 1) % 4], (turn(t, c, 1, 4) + 1) * 16)
                    dve.wait_ge(biased, s)
                    nc.vector.tensor_tensor(core.arena[:, cols(s - 1, D)], part_ring[:, (c - 1) % 4],
                                            x_ring[:, (c - 1) % 4], ALU.add).then_inc(x2_set, 1)
            unrolled(dve, NB + 1, 4, slot, 4, 4)

    row_moments(nc, core, "x2", (), lambda s: core.arena[:, cols(s, D)])
    keep_rows(nc, core, "x2", x2_rows)


def keep_rows(nc, core, name, rows):
    full = core.arena[:, 0:NB * D].rearrange("p (b n) -> p b n", b=NB)
    with ExitStack() as st:
        kept, = sems(nc, st, f"{name}_kept")
        block = st.enter_context(nc.Block())

        @block.sync
        def _(sp):
            for part, out in block_chunks(rows, full, P):
                sp.dma_start(out, part).then_inc(kept, 16)
            sp.wait_ge(kept, 16 * 7)


def feature_norm(nc, core, g0, b0):
    gamma, beta, mean, rstd = (core.hot[:, 2 + n // 2, (n % 2) * 512:(n % 2) * 512 + D] for n in range(4))
    squares = core.work[:, 0:2 * D].rearrange("p (r n) -> p r n", r=2)

    def rows(s):
        return core.arena[:, cols(s, D)]

    def valid(s):
        return TAIL if isinstance(s, int) and s == NB - 1 else P

    with ExitStack() as st:
        (vecs_in, row_set, summed, centred, squared, square_summed, mean_set, var_set, rooted) = sems(
            nc, st, "vecs_in row_set summed centred squared square_summed mean_set var_set rooted0")
        block = st.enter_context(nc.Block())

        @block.sync
        def _(sp):
            sp.dma_start(gamma, g0.partition_broadcast(P)).then_inc(vecs_in, 16)
            sp.dma_start(beta, b0.partition_broadcast(P)).then_inc(vecs_in, 16)

        @block.vector
        def _(dve):
            def norm_rows(s, c, t):
                normalized(nc, core, rows(s), rows(s), s).then_inc(row_set, 1)

            def centre(s, c, t):
                nc.vector.tensor_tensor(rows(s), rows(s), mean, ALU.subtract).then_inc(centred, 1)

            def affine(s, c, t):
                if in_range(s, 0, NB):
                    nc.vector.tensor_tensor(rows(s), rows(s), rstd, ALU.mult)
                if in_range(s, 1, NB + 1):
                    nc.vector.tensor_tensor(rows(s - 1), rows(s - 1), beta, ALU.add)
                dve.drain()
            unrolled(dve, NB, 2, norm_rows, 2, 2)
            dve.wait_ge(summed, NB)
            nc.vector.tensor_scalar(mean, core.bank(0, D), 1.0 / N, None, ALU.mult)
            dve.drain()
            unrolled(dve, NB, 2, centre, 2, 2)
            dve.wait_ge(square_summed, NB)
            nc.vector.tensor_scalar(rstd, core.bank(1, D), 1.0 / N, EPS, ALU.mult, ALU.add).then_inc(var_set, 1)
            dve.wait_ge(rooted, 1)
            nc.vector.reciprocal(rstd, rstd)
            dve.wait_ge(vecs_in, 32)
            dve.drain()
            nc.vector.tensor_tensor(rstd, rstd, gamma, ALU.mult)
            dve.drain()
            unrolled(dve, NB + 1, 2, affine, 2, 2)

        @block.scalar
        def _(act):
            def square(s, c, t):
                act.wait_ge(centred, s + 1)
                ge(act, square_summed, s - 1)
                nc.scalar.activation(squares[:, c], rows(s), ACT.Square).then_inc(squared, 1)
            unrolled(act, NB, 2, square, 2, 2)
            act.wait_ge(var_set, 1)
            nc.scalar.activation(rstd, rstd, ACT.Sqrt).then_inc(rooted, 1)

        @block.tensor
        def _(pe):
            def add_rows(s, c, t):
                pe.wait_ge(row_set, s + 1)
                nc.tensor.matmul(core.bank(0, D), core.ones[0:valid(s), :], rows(s)[0:valid(s)],
                                 start=isinstance(s, int) and s == 0, stop=isinstance(s, int) and s == NB - 1)\
                    .then_inc(summed, 1)

            def add_squares(s, c, t):
                pe.wait_ge(squared, s + 1)
                nc.tensor.matmul(core.bank(1, D), core.ones[0:valid(s), :], squares[0:valid(s), c],
                                 start=isinstance(s, int) and s == 0, stop=isinstance(s, int) and s == NB - 1)\
                    .then_inc(square_summed, 1)
            unrolled(pe, NB, 2, add_rows, 2, 2)
            unrolled(pe, NB, 2, add_squares, 2, 2)


def gin_layer(nc, core, name, wa, ba, gamma, beta, wb, bb):
    PAIRS = -(-NB // 2)
    w_a = core.hot[:, 0, 0:2 * D].rearrange("p (k n) -> p k n", k=2)
    w_b = core.hot[:, 0, 2 * D:4 * D].rearrange("p (k n) -> p k n", k=2)
    vecs = core.hot[:, 1, 0:6].rearrange("p (v k) -> p v k", v=3)
    bias = core.hot[:, 1, 8:8 + D]
    agg = core.hot[:, 1, 300:304].rearrange("p (k n) -> p k n", k=2)
    scale, shift, std = (core.hot[:, 1, 304 + 2 * n:306 + 2 * n] for n in range(3))
    stats = core.hot[:, 2, 0:2 * PAIRS * 6].rearrange("p (k q n) -> p k q n", k=2, q=PAIRS)
    u = core.work[:, 0:4 * D].rearrange("p (r n) -> p r n", r=4)
    ut = core.work[:, 4 * D:8 * D].rearrange("p (r k n) -> p r k n", r=2, k=2)
    rt = core.work[:, 8 * D:12 * D].rearrange("p (r k n) -> p r k n", r=2, k=2)

    def hidden(q, k, n=None):
        return core.arena[:, cols(q, 2 * D, AGG0 + k * blocks(q) * P, n or blocks(q) * P)]

    def width(q):
        return TAIL if isinstance(q, int) and q == PAIRS - 1 else D

    def blocks(q):
        return 1 if isinstance(q, int) and q == PAIRS - 1 else 2

    with ExitStack() as st:
        weights_in, u_set, u_turned, ut_copied, product, hid_set, stats_set = sems(
            nc, st, " ".join(f"{name}_{n}" for n in "weights_in u_set u_turned ut_copied product hid_set stats_set".split()))
        block = st.enter_context(nc.Block())

        @block.sync
        def _(sp):
            for t, a in ((w_a, wa.rearrange("(k p) n -> p k n", p=P)), (w_b, wb.rearrange("(k p) n -> p k n", p=P)),
                         (vecs[:, 0], ba), (vecs[:, 1], gamma),
                         (vecs[:, 2], beta), (bias, bb.partition_broadcast(P))):
                sp.dma_start(t, a).then_inc(weights_in, 16)

        @block.vector
        def _(dve):
            def slot(s, c, t):
                if in_range(s, 0, PAIRS):
                    ge(dve, u_turned, 2 * (s - 1))
                    for i in range(blocks(s)):
                        nc.vector.tensor_tensor(u[:, 2 * c + i], core.arena[:, cols(s, 2 * D, i * D, D)],
                                                core.arena[:, cols(s, 2 * ACW, AGG0 + i * ACW, D)], ALU.add)\
                            .then_inc(u_set, 1)
                if in_range(s, 2, PAIRS + 2):
                    g = s - 2
                    dve.wait_ge(hid_set, s - 1)
                    for k in range(2):
                        last = nc.vector.bn_stats(stats[:, k, bass.ds(g, 1)].rearrange("p o n -> p (o n)"),
                                                  hidden(g, k, width(g)))
                    last.then_inc(stats_set, 1)
            unrolled(dve, PAIRS + 2, 2, slot, 2, 4)
            dve.wait_ge(stats_set, PAIRS)
            for k in range(2):
                nc.vector.bn_aggr(agg[:, k], stats[:, k])
            dve.drain()
            nc.vector.tensor_scalar(std, agg[:, :, 1], EPS, None, ALU.add)

        @block.tensor
        def _(pe):
            def slot(s, c, t):
                if in_range(s, 0, PAIRS):
                    ge(pe, ut_copied, s - 1)
                    for i in range(blocks(s)):
                        pe.wait_ge(u_set, 2 * s + i + 1)
                        for k in range(2):
                            last = nc.tensor.transpose(core.bank(c)[:, k * D + i * P:k * D + (i + 1) * P],
                                                       u[:, 2 * c + i, k * P:(k + 1) * P], core.ident[:])
                        last.then_inc(u_turned, 1)
                if in_range(s, 1, PAIRS + 1):
                    r, n = (c + 1) % 2, blocks(s - 1) * P
                    if isinstance(s, int) and s == 1:
                        pe.wait_ge(weights_in, 96)
                    pe.wait_ge(ut_copied, s)
                    ge(pe, hid_set, s - 2)
                    for m in range(2):
                        for k in range(2):
                            last = nc.tensor.matmul(core.bank(2 + r)[:, m * D:m * D + n], w_a[:, k, m * P:(m + 1) * P],
                                                    ut[:, r, k, 0:n], start=(k == 0), stop=(k == 1))
                    last.then_inc(product, 1)
            unrolled(pe, PAIRS + 1, 2, slot, 2, 3)

        @block.scalar
        def _(act):
            act.wait_ge(weights_in, 96)

            def slot(s, c, t):
                if in_range(s, 0, PAIRS):
                    n = blocks(s) * P
                    act.wait_ge(u_turned, 2 * s + blocks(s))
                    ge(act, product, s - 1)
                    nc.scalar.activation(ut[:, c, :, 0:n], core.bank(c).rearrange("p (k n) -> p k n", k=2)[:, :, 0:n],
                                         ACT.Copy).then_inc(ut_copied, 1)
                if in_range(s, 1, PAIRS + 1):
                    n = blocks(s - 1) * P
                    act.wait_ge(product, s)
                    for m in range(2):
                        last = nc.scalar.activation(hidden(s - 1, m), core.bank(2 + (c + 1) % 2)[:, m * D:m * D + n],
                                                    ACT.Identity, bias=vecs[:, 0, m:m + 1])
                    last.then_inc(hid_set, 1)
            unrolled(act, PAIRS + 1, 2, slot, 2, 3)

    with ExitStack() as st:
        rooted, affine_set, r_set, product, biased = sems(
            nc, st, " ".join(f"{name}_{n}" for n in "rooted affine_set r_set product2 biased".split()))
        block = st.enter_context(nc.Block())

        @block.scalar
        def _(act):
            nc.scalar.activation(std, std, ACT.Sqrt).then_inc(rooted, 1)
            act.wait_ge(affine_set, 1)

            def slot(s, c, t):
                if in_range(s, 0, PAIRS):
                    n = blocks(s) * P
                    ge(act, product, 2 * (s - 1))
                    for k in range(2):
                        last = nc.scalar.activation(rt[:, c, k, 0:n], hidden(s, k), ACT.Relu,
                                                    scale=scale[:, k:k + 1], bias=shift[:, k:k + 1])
                    last.then_inc(r_set, 1)
                if in_range(s, 1, PAIRS + 1):
                    for i in range(blocks(s - 1)):
                        act.wait_ge(biased, 2 * (s - 1) + i + 1)
                        out = core.arena[:, cols(s - 1, 2 * D, i * D, D)]
                        nc.scalar.activation(out, out, ACT.Relu)
            unrolled(act, PAIRS + 1, 2, slot, 2, 3)

        @block.vector
        def _(dve):
            dve.wait_ge(rooted, 1)
            nc.vector.reciprocal(scale, std)
            dve.drain()
            nc.vector.tensor_tensor(scale, scale, vecs[:, 1], ALU.mult)
            dve.drain()
            nc.vector.tensor_tensor(shift, scale, agg[:, :, 0], ALU.mult)
            dve.drain()
            nc.vector.tensor_tensor(shift, vecs[:, 2], shift, ALU.subtract).then_inc(affine_set, 1)

            def slot(s, c, t):
                for i in range(blocks(s)):
                    dve.wait_ge(product, 2 * s + i + 1)
                    nc.vector.tensor_tensor(core.arena[:, cols(s, 2 * D, i * D, D)], core.bank(2 * c + i, D), bias, ALU.add)\
                        .then_inc(biased, 1)
            unrolled(dve, PAIRS, 2, slot, 2, 3)

        @block.tensor
        def _(pe):
            def slot(s, c, t):
                pe.wait_ge(r_set, s + 1)
                ge(pe, biased, 2 * (s - 1))
                for i in range(blocks(s)):
                    for k in range(2):
                        last = nc.tensor.matmul(core.bank(2 * c + i, D), rt[:, c, k, i * P:(i + 1) * P], w_b[:, k],
                                                start=(k == 0), stop=(k == 1))
                    last.then_inc(product, 1)
            unrolled(pe, PAIRS, 2, slot, 2, 3)


def output_rows(nc, core, x2_rows, weight_t, bias, out):
    w = core.hot[:, 0, 0:2 * D].rearrange("p (k n) -> p k n", k=2)
    b_wide = core.hot[:, 1, 0:D]
    high = core.arena[:, AGG0:ARENA].rearrange("p (b n) -> p b n", b=NB)[:, :, 0:D]
    rows = core.work[:, 8 * D:10 * D].rearrange("p (r n) -> p r n", r=2)
    parts = core.work[:, 10 * D:11 * D]
    with ExitStack() as st:
        weights_in, x_in = sems(nc, st, "out_weights_in x2_in")
        block = st.enter_context(nc.Block())

        @block.sync
        def _(sp):
            sp.dma_start(w, weight_t.rearrange("(k p) n -> p k n", p=P)).then_inc(weights_in, 16)
            sp.dma_start(b_wide, bias.partition_broadcast(P)).then_inc(weights_in, 16)
            for part, rows_ in block_chunks(x2_rows, high, P):
                sp.dma_start(part, rows_).then_inc(x_in, 16)
            sp.wait_ge(weights_in, 32)
            sp.wait_ge(x_in, 16 * 7)

    def place(s):
        return core.arena[:, cols(s, ACW, AGG0, D)]

    def add_rows(dve, s, r):
        nc.vector.tensor_tensor(place(s), place(s), core.arena[:, cols(s, D)], ALU.add)

    row_moments(nc, core, "x3", (add_rows,), place)

    def prepare(dve, s, tile, r, _):
        return normalized(nc, core, tile, place(s), s)

    def finish(dve, s, prod, r):
        nc.vector.tensor_tensor(rows[:, r], prod, b_wide, ALU.add)
        dve.drain()
        return nc.vector.tensor_tensor(rows[:, r], rows[:, r], place(s), ALU.add)

    def store(sp, s, r):
        n = TAIL if isinstance(s, int) and s == NB - 1 else P
        return sp.dma_start(out[bass.ds(s * P, n), :], rows[0:n, r])

    dense_tiles(nc, "out", core, [w[:, 0], w[:, 1]], D, None, prepare, finish, store)


def gnn_program(nc, a, out):
    def dram(name, width):
        return nc.dram_tensor(name, (NPAD, width), F32).ap()

    rows1, rows2, rows3 = dram("rows_gat1", ROW1), dram("rows_gat2", ROW2), dram("rows_gin", D)
    rows4, x1_rows, x2_rows = dram("rows_gin2", D), dram("x1_rows", D), dram("x2_rows", D)
    with ExitStack() as st:
        core = Core(nc, st)
        set_constants(nc, core)
        plan_steps(nc, core, a["src"], a["dst"])
        gat1_tables(nc, core, a["x"], a["L0_gnn_W1"], a["L0_gnn_al1"], a["L0_gnn_ar1"], rows1)
        spread_attention(nc, core, H1)
        edge_pass(nc, core, "e1", rows1, ROW1, H1, True)
        gat2_tables(nc, core, a["L0_gnn_W2"], a["L0_gnn_al2"], a["L0_gnn_ar2"], a["L0_gnn_b1"], rows2)
        spread_attention(nc, core, 1)
        edge_pass(nc, core, "e2", rows2, ROW2, 1, True)
        first_residual(nc, core, a["x"], a["L0_gnn_b2"], x1_rows)
        wl = core.hot[:, 0].rearrange("p (k n) -> p k n", k=2)
        bl = core.hot[:, 1, 0:NH * NSL]
        slice_logits(nc, core, a["w_xt"], a["b_xt"], a["L0_ffn_W_slice"], a["L0_ffn_b_slice"], a["temperature"], wl, bl)
        total = slice_weights(nc, core, wl, bl)
        v2 = core.hot[:, 0].rearrange("p (j n) -> p j n", j=NH // 2)
        slice_attention(nc, core, total, a["L0_ffn_W_fx"], a["b_fxt"], a["L0_ffn_W_q"], a["L0_ffn_W_k"], a["L0_ffn_W_v"],
                        a["L0_ffn_W_out"], v2)
        second_residual(nc, core, v2, a["L0_ffn_b_out"], x1_rows, x2_rows)
        feature_norm(nc, core, a["L1_gnn_g0"], a["L1_gnn_b0"])
        keep_rows(nc, core, "h0", rows3)
        edge_pass(nc, core, "e3", rows3, D, 1, False)
        gin_layer(nc, core, "n1", *(a["L1_gnn_" + n] for n in ("W1a", "b1a", "g1", "bt1", "W1b", "b1b")))
        keep_rows(nc, core, "h1", rows4)
        edge_pass(nc, core, "e4", rows4, D, 1, False)
        gin_layer(nc, core, "n2", *(a["L1_gnn_" + n] for n in ("W2a", "b2a", "g2", "bt2", "W2b", "b2b")))
        output_rows(nc, core, x2_rows, a["weight_t"], a["L1_ffn_bias"], out)


def kernel(**inputs):
    import concourse.bacc as bacc
    from concourse.bass_utils import run_bass_kernel_spmd

    nc = bacc.Bacc("TRN2", target_bir_lowering=False, num_devices=1)
    laid = {n: np.asarray(v) for n, v in inputs.items()}
    laid["w_xt"] = laid.pop("L0_ffn_W_x").T
    laid["b_xt"] = laid.pop("L0_ffn_b_x").reshape(NH, DH).T
    laid["b_fxt"] = laid.pop("L0_ffn_b_fx").reshape(NH, DH).T
    laid["temperature"] = laid.pop("L0_ffn_temperature").reshape(NH)
    laid["weight_t"] = laid.pop("L1_ffn_weight").T
    for n in "b1a g1 bt1 b2a g2 bt2".split():
        laid["L1_gnn_" + n] = laid["L1_gnn_" + n].reshape(D // P, P).T
    arrays, views = {}, {}
    for name, value in laid.items():
        arrays[name] = np.ascontiguousarray(value)
        views[name] = nc.dram_tensor(name, value.shape, mybir.dt.from_np(value.dtype), kind="ExternalInput").ap()
    out = nc.dram_tensor("out", (N, D), F32, kind="ExternalOutput").ap()
    gnn_program(nc, views, out)
    result = run_bass_kernel_spmd(nc, [arrays], core_ids=[0])
    return result.results[0]["out"]
```

```python
import numpy as np
from contextlib import ExitStack

import concourse.bass as bass
from concourse import mybir

F32 = mybir.dt.float32
BF16 = mybir.dt.bfloat16
I32 = mybir.dt.int32
ALU = mybir.AluOpType
ACT = mybir.ActivationFunctionType
AX = mybir.AxisListType

N = 6250
D = 256
E = 106250
P = 128
NB = -(-N // P)
TAIL = N - (NB - 1) * P
NPAD = NB * P
EP, EC = 125, 850
ET = EC
EPAD = ET * P - E
PADP, PADC = 102, 25
GS = 8
NG = -(-(-(-E // P) + NB) // GS)
RING = 4
TC = -(-NG * GS // P)
SK = TC * P
H1 = 2
HD = D // H1
ROW1 = D + 2 * H1
ROW2 = D + 2
ACW = D + H1
FAR = 1.0e30
EPS = 1e-5
SLOPE = 0.2
NH, DH, NSL = 8, 64, 64
INNER = NH * DH
ARENA = 25700
AGG0 = ARENA - NB * ACW
PAD_DST = 1 << 20


def unrolled(eng, total, unroll, body, head, tail):
    turns = (total - head - tail) // unroll
    for s in range(head):
        body(s, s % unroll, s // unroll)
    if turns > 0:
        assert head % unroll == 0
        with eng.Fori(head // unroll, head // unroll + turns) as it:
            for c in range(unroll):
                body(it * unroll + c, c, it)
    for s in range(head + max(turns, 0) * unroll, total):
        body(s, s % unroll, s // unroll)


def turn(t, c, back, unroll):
    return t + (c - back) // unroll


def in_range(s, lo, hi):
    return not isinstance(s, int) or lo <= s < hi


def ge(eng, sem, value):
    if isinstance(value, int) and value <= 0:
        return
    eng.wait_ge(sem, value)


class Core:

    def __init__(self, nc, stack):
        self.nc, self.stack = nc, stack
        self.arena = self.sb("arena", [P, ARENA])
        self.work = self.sb("work", [P, RING * GS * ROW1])
        self.hot = self.sb("hot", [P, RING, GS * P])
        self.ident = self.sb("ident", [P, P])
        self.ones = self.sb("ones", [P, P])
        self.iota_col = self.sb("iota_col", [P, P])
        self.part = self.sb("part", [P, 1])
        self.step_idx = self.sb("step_idx", [P, SK], I32)
        self.step_dst = self.sb("step_dst", [P, SK])
        self.step_same = self.sb("step_same", [P, SK])
        self.step_reset = self.sb("step_reset", [P, SK])
        self.step_sel = self.sb("step_sel", [NB, SK])
        self.unordered = self.sb("unordered", [1, 1], I32)
        self.step_at = self.sb("step_at", [1, SK], I32)
        self.er = self.sb("er", [P, H1, NB])
        self.el = self.sb("el", [P, H1, NB])
        self.er_steps = self.sb("er_steps", [P, H1, SK])
        self.er_parts = self.sb("er_parts", [P, 3, H1, SK], BF16)
        self.low = self.sb("low", [P, 2])
        self.moments = self.sb("moments", [P, NB, 10])
        self.idx_ring = self.sb("idx_ring", [P, RING, GS], I32)
        self.psum = stack.enter_context(nc.psum_tensor("psum", [P, 4096], F32))
        self.dl_rows = nc.dram_tensor("dl_rows", (SK, P), BF16).ap()

    def sb(self, name, shape, dt=F32):
        return self.stack.enter_context(self.nc.sbuf_tensor(name, shape, dt))

    def bank(self, n, width=512):
        return self.psum[:, n * 512:n * 512 + width]

    def agg(self, b):
        return self.arena[:, AGG0 + b * ACW:AGG0 + (b + 1) * ACW]


def sems(nc, stack, names):
    made = [stack.enter_context(nc.semaphore(n)) for n in names.split()]
    start = made[0].num
    for before, after in zip(made, made[1:] + [None]):
        if after is None or after.num != before.num + 1:
            stack.callback(nc.gpsimd.sem_clear, range(start, before.num + 1))
            start = after.num if after is not None else 0
    return made


def ring_sems(nc, stack, name, count):
    return sems(nc, stack, " ".join(f"{name}{r}" for r in range(count)))


def set_constants(nc, core):
    with ExitStack() as st:
        zeroed, = sems(nc, st, "ident_zeroed")
        block = st.enter_context(nc.Block())

        @block.gpsimd
        def _(pool):
            nc.gpsimd.memset(core.ident[:], 0.0).then_inc(zeroed, 1)
            nc.gpsimd.iota(core.iota_col[:], pattern=[[1, P]], base=0, channel_multiplier=0,
                           allow_small_or_imprecise_dtypes=True)
            nc.gpsimd.iota(core.part[:], pattern=[[0, 1]], base=0, channel_multiplier=1,
                           allow_small_or_imprecise_dtypes=True)
            pool.wait_ge(zeroed, 1)
            nc.gpsimd.affine_select(out=core.ident[:], in_=core.ident[:], compare_op=ALU.not_equal, fill=1.0,
                                    base=0, pattern=[[-1, P]], channel_multiplier=1)

        @block.vector
        def _(dve):
            nc.vector.memset(core.ones[:], 1.0)


def plan_steps(nc, core, src, dst):
    src_rows = nc.dram_tensor("src_rows", (ET, P), I32).ap()
    dst_rows = nc.dram_tensor("dst_rows", (ET, P), I32).ap()
    at = [0]

    def scratch(cols, dt=F32):
        view = core.arena[:, at[0]:at[0] + cols]
        at[0] += cols
        return view if dt == F32 else view.bitcast(dt)

    e_src, e_dst, e_next = scratch(EC, I32), scratch(EC, I32), scratch(EC, I32)
    blk_i, next_i, blk = scratch(EC, I32), scratch(EC, I32), scratch(EC // 2, BF16)
    disorder, any_disorder = scratch(1), scratch(1)
    less = scratch(EC // 2, BF16)
    pad = scratch(2 * PADC, I32)
    below = scratch(NB)
    bound, bound_i = scratch(1), scratch(1, I32)
    k_idx, reached, brow, trow = scratch(SK), scratch(SK), scratch(SK), scratch(SK)
    tile_i, blk_off = scratch(TC, I32), scratch(TC)
    g_src, g_dst = scratch(SK, I32), scratch(SK, I32)
    f_src, f_dst, b_dst = scratch(SK), scratch(SK), scratch(SK // 2, BF16)
    assert at[0] <= AGG0

    def flat(t, lo, hi, parts):
        return t.rearrange("r e -> (r e)")[lo:hi].rearrange("(p c) -> p c", p=parts)

    with ExitStack() as st:
        edges_in, pad_set, rows_out, next_in, counted = sems(nc, st, "edges_in pad_set rows_out next_in counted")
        block = st.enter_context(nc.Block())

        @block.sync
        def _(sp):
            sp.dma_start(e_dst[0:EP, :], dst.rearrange("(p c) -> p c", p=EP)).then_inc(edges_in, 16)
            sp.dma_start(e_src[0:EP, :], src.rearrange("(p c) -> p c", p=EP)).then_inc(edges_in, 16)
            sp.wait_ge(edges_in, 32)
            sp.dma_start(flat(dst_rows, 0, E, EP), e_dst[0:EP, :]).then_inc(rows_out, 16)
            sp.dma_start(flat(src_rows, 0, E, EP), e_src[0:EP, :]).then_inc(rows_out, 16)
            sp.wait_ge(pad_set, 2)
            sp.dma_start(flat(dst_rows, E, ET * P, PADP), pad[0:PADP, 0:PADC]).then_inc(rows_out, 16)
            sp.dma_start(flat(src_rows, E, ET * P, PADP), pad[0:PADP, PADC:]).then_inc(rows_out, 16)
            sp.wait_ge(rows_out, 64)
            sp.dma_start(e_next[0:EP, :], flat(dst_rows, 1, E + 1, EP)).then_inc(next_in, 16)

        @block.gpsimd
        def _(pool):
            nc.gpsimd.memset(pad[:, 0:PADC], PAD_DST).then_inc(pad_set, 1)
            nc.gpsimd.memset(pad[:, PADC:], 0).then_inc(pad_set, 1)
            nc.gpsimd.memset(core.arena[:, AGG0:ARENA], 0.0)
            nc.gpsimd.iota(k_idx, pattern=[[1, SK]], base=0, channel_multiplier=0,
                           allow_small_or_imprecise_dtypes=True)

        @block.vector
        def _(dve):
            nc.vector.memset(below[:, 0:1], 0.0)
            dve.wait_ge(edges_in, 32)
            nc.vector.tensor_single_scalar(blk_i[0:EP, :], e_dst[0:EP, :], P.bit_length() - 1, ALU.arith_shift_right)
            dve.drain()
            nc.vector.tensor_copy(blk[0:EP, :], blk_i[0:EP, :])
            for b in range(1, NB):
                dve.drain()
                nc.vector.tensor_scalar(less[0:EP, :], blk[0:EP, :], float(b), 0.0, ALU.is_lt, ALU.add,
                                        accum_out=below[0:EP, b:b + 1])
            dve.wait_ge(next_in, 16)
            nc.vector.tensor_single_scalar(next_i[0:EP, :], e_next[0:EP, :], P.bit_length() - 1, ALU.arith_shift_right)
            dve.drain()
            nc.vector.tensor_tensor(next_i[0:EP, :], blk_i[0:EP, :], next_i[0:EP, :], ALU.is_gt)
            dve.drain()
            nc.vector.tensor_reduce(disorder[0:EP, :], next_i[0:EP, :], AX.X, ALU.max)
            dve.drain()
            nc.vector.memset(bound, 0.0).then_inc(counted, 1)

        @block.tensor
        def _(pe):
            pe.wait_ge(counted, 1)
            nc.tensor.matmul(core.bank(0, 1)[0:NB, :], below[0:EP, 0:NB], core.ones[0:EP, 0:1], start=True, stop=True)
            nc.tensor.matmul(core.bank(3, 1)[0:1, :], disorder[0:EP, :], core.ones[0:EP, 0:1], start=True, stop=True)

    with ExitStack() as st:
        reached_set, brow_summed = sems(nc, st, "reached_set brow_summed")
        block = st.enter_context(nc.Block())

        @block.vector
        def _(dve):
            nc.vector.tensor_copy(bound_i[0:NB, :], core.bank(0, 1)[0:NB, :])
            nc.vector.tensor_scalar(core.unordered[:], core.bank(3, 1)[0:1, :], 1.0, None, ALU.min)
            dve.drain()
            nc.vector.tensor_single_scalar(tile_i[0:NB, 0:1], bound_i[0:NB, :], P.bit_length() - 1, ALU.arith_shift_right)
            dve.drain()
            nc.vector.tensor_copy(blk_off[0:NB, 0:1], tile_i[0:NB, 0:1])
            dve.drain()
            nc.vector.tensor_tensor(bound[0:NB, :], blk_off[0:NB, 0:1], core.part[0:NB, :], ALU.add)
            dve.drain()
            nc.vector.tensor_scalar(reached[0:NB, :], k_idx[0:NB, :], bound[0:NB, 0:1], None, ALU.is_ge)\
                .then_inc(reached_set, 1)
            dve.wait_ge(brow_summed, 1)
            nc.vector.tensor_scalar(brow, core.psum[:, 512:512 + 2 * 512].rearrange("p (a k) -> p a k", a=2)
                                    [:, :, 0:SK // 2], -1.0, None, ALU.add)
            dve.drain()
            nc.vector.tensor_tensor(trow, k_idx, brow, ALU.subtract)
            nc.vector.tensor_tensor(core.step_same[:, 1:SK], brow[:, 1:SK], brow[:, 0:SK - 1], ALU.is_equal)
            nc.vector.memset(core.step_same[:, 0:1], 0.0)
            nc.vector.tensor_scalar(core.step_at[:], brow[0:1, :], float(ACW), float(AGG0), ALU.mult, ALU.add)
            nc.vector.tensor_scalar(core.step_sel[:], brow[0:NB, :], core.part[0:NB, 0:1], None, ALU.is_equal)
            dve.drain()
            nc.vector.tensor_scalar(core.step_reset[:], core.step_same[:], -1.0, FAR, ALU.add, ALU.mult)

        @block.tensor
        def _(pe):
            pe.wait_ge(reached_set, 1)
            for a in range(2):
                last = nc.tensor.matmul(core.bank(1 + a, SK // 2), core.ones[0:NB, :],
                                        reached[0:NB, a * (SK // 2):(a + 1) * (SK // 2)], start=True, stop=True)
            last.then_inc(brow_summed, 1)

    bucket_edges(nc, core, src_rows, dst_rows, below)

    with ExitStack() as st:
        turned, tiles_set, shifted, flipped, kept = sems(nc, st, "turned tiles_set shifted flipped kept")
        rows_in = core.stack.enter_context(nc.semaphore("plan_rows_in"))
        block = st.enter_context(nc.Block())
        t_ps, b_ps = core.bank(0, TC), core.bank(1, TC)

        @block.tensor
        def _(pe):
            for c in range(TC):
                nc.tensor.matmul(t_ps[:, c:c + 1], trow[0:1, c * P:(c + 1) * P], core.ones[0:1, 0:1], start=True, stop=True)
                last = nc.tensor.matmul(b_ps[:, c:c + 1], brow[0:1, c * P:(c + 1) * P], core.ones[0:1, 0:1],
                                        start=True, stop=True)
            last.then_inc(turned, 1)
            pe.wait_ge(shifted, 1)
            for n, rows in enumerate((f_src, f_dst)):
                for c in range(TC):
                    last = nc.tensor.transpose(core.psum[:, (2 + 2 * n) * 512 + c * P:(2 + 2 * n) * 512 + (c + 1) * P],
                                               rows[:, c * P:(c + 1) * P], core.ident[:])
            last.then_inc(flipped, 1)

        @block.gpsimd
        def _(pool):
            pool.wait_ge(tiles_set, 1)
            pool.nop(nofuse=True)
            for c in range(TC):
                for rows, table in ((g_src, src_rows), (g_dst, dst_rows)):
                    nc.gpsimd.indirect_dma_start(
                        rows[:, c * P:(c + 1) * P], None, table,
                        bass.IndirectOffsetOnAxis(ap=tile_i[:, c:c + 1], axis=0)).then_inc(rows_in, 16)

        @block.vector
        def _(dve):
            dve.wait_ge(turned, 1)
            nc.vector.tensor_copy(tile_i[:, 0:TC], t_ps).then_inc(tiles_set, 1)
            nc.vector.tensor_scalar(blk_off[:, 0:TC], b_ps, float(P), None, ALU.mult)
            dve.wait_ge(rows_in, 32 * TC)
            nc.vector.tensor_copy(f_src, g_src)
            nc.vector.tensor_copy(f_dst, g_dst)
            dve.drain()
            for c in range(TC):
                nc.vector.tensor_scalar(f_dst[:, c * P:(c + 1) * P], f_dst[:, c * P:(c + 1) * P],
                                        blk_off[:, c:c + 1], None, ALU.subtract)
            dve.drain()
            nc.vector.tensor_copy(b_dst, f_dst).then_inc(shifted, 1)
            dve.wait_ge(flipped, 1)
            nc.vector.tensor_copy(core.step_idx[:], core.psum[:, 2 * 512:2 * 512 + SK])
            nc.vector.tensor_copy(core.step_dst[:], core.psum[:, 4 * 512:4 * 512 + SK])

        @block.sync
        def _(sp):
            sp.wait_ge(shifted, 1)
            sp.dma_start(core.dl_rows.rearrange("(c p) e -> p c e", p=P),
                         b_dst.rearrange("p (c e) -> p c e", e=P)).then_inc(kept, 16)
            sp.wait_ge(kept, 16)


def bucket_edges(nc, core, src_rows, dst_rows, below):
    ROWS = -(-E // P)
    BU = NB + 1
    at = [0]

    def scratch(cols, dt=F32):
        view = core.work[:, at[0]:at[0] + cols]
        at[0] += cols
        return view if dt == F32 else view.bitcast(dt)

    rows_i = scratch(SK, I32), scratch(SK, I32)
    rows_f = scratch(SK), scratch(SK)
    edge = scratch(SK), scratch(SK)
    blk, blk_i = scratch(SK), scratch(SK, I32)
    earlier, free = scratch(P), scratch(BU)
    hot, place, hit, spot = scratch(BU), scratch(BU), scratch(BU), scratch(1)
    spot_i, pay = scratch(1, I32), (scratch(1, I32), scratch(1, I32))
    assert at[0] <= RING * GS * ROW1
    with ExitStack() as st:
        rows_in, converted, turned, hot_set, ranked, spots_set = sems(
            nc, st, " ".join("bucket_" + n for n in "rows_in converted turned hot_set ranked spots_set".split()))
        placed = [core.stack.enter_context(nc.semaphore(f"edges_placed{n}")) for n in range(2)]
        block = st.enter_context(nc.Block())

        def flag(eng):
            return eng.value_load(core.unordered[0:1, 0:1])

        @block.sync
        def _(sp):
            with sp.If(flag(sp) > 0):
                for view, rows in zip(rows_i, (src_rows, dst_rows)):
                    for c in range(TC):
                        n = min(P, ET - c * P)
                        if c == TC - 1:
                            sp.wait_ge(hot_set, 1)
                        sp.dma_start(view[0:n, c * P:(c + 1) * P], rows[c * P:c * P + n, :]).then_inc(rows_in, 16)

        @block.vector
        def _(dve):
            def slot(s, c, t):
                nc.vector.tensor_scalar(hot, core.iota_col[:, 0:BU], blk[:, bass.ds(s, 1)], None, ALU.is_equal)\
                    .then_inc(hot_set, 1)
                dve.wait_ge(ranked, s + 1)
                nc.vector.tensor_tensor(place, core.bank(6, BU), free, ALU.add)
                dve.drain()
                nc.vector.tensor_tensor(hit, place, hot, ALU.mult)
                nc.vector.tensor_tensor(free, core.bank(7, BU), free, ALU.add)
                dve.drain()
                nc.vector.tensor_reduce(spot, hit, AX.X, ALU.add)
                dve.drain()
                for n in range(2):
                    ge(dve, placed[n], s * 16)
                    nc.vector.tensor_copy(pay[n], edge[n][:, bass.ds(s, 1)])
                nc.vector.tensor_copy(spot_i, spot)
                dve.drain()
                dve.sem_inc(spots_set, 1)

            with dve.If(flag(dve) > 0):
                for view in rows_i:
                    nc.vector.memset(view[:, (TC - 1) * P:], 0)
                dve.drain()
                nc.vector.tensor_scalar(earlier, core.iota_col[:], core.part[:, 0:1], None, ALU.is_gt).then_inc(hot_set, 1)
                dve.wait_ge(rows_in, 32 * TC)
                for n in range(2):
                    last = nc.vector.tensor_copy(rows_f[n], rows_i[n])
                last.then_inc(converted, 1)
                dve.wait_ge(turned, 1)
                for n in range(2):
                    nc.vector.tensor_copy(edge[n], core.psum[:, (2 + 2 * n) * 512:(2 + 2 * n) * 512 + SK])
                dve.drain()
                nc.vector.tensor_copy(rows_i[0], edge[1])
                dve.drain()
                nc.vector.tensor_single_scalar(blk_i, rows_i[0], P.bit_length() - 1, ALU.arith_shift_right)
                dve.drain()
                nc.vector.tensor_scalar(blk, blk_i, float(NB), None, ALU.min)
                nc.vector.tensor_copy(free[:, 0:NB], core.bank(1, NB))
                nc.vector.memset(free[:, NB:BU], float(E))
                dve.drain()
                unrolled(dve, ROWS, 1, slot, 1, 1)

        @block.tensor
        def _(pe):
            def slot(s, c, t):
                pe.wait_ge(hot_set, s + 2)
                nc.tensor.matmul(core.bank(6, BU), earlier, hot, start=True, stop=True)
                nc.tensor.matmul(core.bank(7, BU), core.ones[:], hot, start=True, stop=True).then_inc(ranked, 1)

            with pe.If(flag(pe) > 0):
                nc.tensor.matmul(core.bank(1, NB), core.ones[0:EP, :], below[0:EP, 0:NB], start=True, stop=True)
                pe.wait_ge(converted, 1)
                for n in range(2):
                    for c in range(TC):
                        last = nc.tensor.transpose(
                            core.psum[:, (2 + 2 * n) * 512 + c * P:(2 + 2 * n) * 512 + (c + 1) * P],
                            rows_f[n][:, c * P:(c + 1) * P], core.ident[:])
                last.then_inc(turned, 1)
                unrolled(pe, ROWS, 1, slot, 1, 1)

        @block.gpsimd
        def _(pool):
            def slot(s, c, t):
                pool.wait_ge(spots_set, s + 1)
                pool.nop(nofuse=True)
                for n, rows in enumerate((src_rows, dst_rows)):
                    nc.gpsimd.indirect_dma_start(
                        rows.rearrange("r (e o) -> (r e) o", o=1), bass.IndirectOffsetOnAxis(ap=spot_i[:, 0:1], axis=0),
                        pay[n], None).then_inc(placed[n], 16)

            with pool.If(flag(pool) > 0):
                unrolled(pool, ROWS, 1, slot, 1, 1)
                for n in range(2):
                    pool.wait_ge(placed[n], ROWS * 16)


def dense_tiles(nc, name, core, weights, width, prepare, finish, store, func=ACT.Copy):
    lhs = core.work[:, 0:4 * D].rearrange("p (r c f) -> p r c f", r=4, c=2)
    turned = core.work[:, 4 * D:8 * D].rearrange("p (r c f) -> p r c f", r=4, c=2)
    SLOTS = NB + 3
    with ExitStack() as st:
        tile_set, tile_turned, tile_copied, product, product_used = sems(
            nc, st, " ".join(f"{name}_{x}" for x in "tile tile_turned tile_copied product product_used".split()))
        stored = ring_sems(nc, st, f"{name}_stored", 4)
        block = st.enter_context(nc.Block())

        @block.vector
        def _(dve):
            def slot(s, c, t):
                if in_range(s, 0, NB):
                    ge(dve, tile_turned, s - 3)
                    prepare(dve, s, lhs[:, c].rearrange("p c f -> p (c f)")).then_inc(tile_set, 1)
                if in_range(s, 3, SLOTS):
                    dve.wait_ge(product, s - 2)
                    ge(dve, stored[(c - 3) % 4], turn(t, c, 3, 4) * 16)
                    finish(dve, s - 3, core.bank(4 + (c - 3) % 4, width), (c - 3) % 4).then_inc(product_used, 1)
            unrolled(dve, SLOTS, 4, slot, 8, 4)

        @block.tensor
        def _(pe):
            def slot(s, c, t):
                if in_range(s, 0, NB):
                    pe.wait_ge(tile_set, s + 1)
                    ge(pe, tile_copied, s - 3)
                    for k in range(2):
                        last = nc.tensor.transpose(core.bank(c)[:, k * P:(k + 1) * P], lhs[:, c, k], core.ident[:])
                    last.then_inc(tile_turned, 1)
                if in_range(s, 2, NB + 2):
                    r = (c - 2) % 4
                    pe.wait_ge(tile_copied, s - 1)
                    ge(pe, product_used, s - 5)
                    for k in range(2):
                        last = nc.tensor.matmul(core.bank(4 + r, width), turned[:, r, k], weights[k],
                                                start=(k == 0), stop=(k == 1))
                    last.then_inc(product, 1)
            unrolled(pe, NB + 2, 4, slot, 8, 4)

        @block.scalar
        def _(act):
            def slot(s, c, t):
                act.wait_ge(tile_turned, s + 1)
                ge(act, product, s - 3)
                nc.scalar.activation(turned[:, c].rearrange("p c f -> p (c f)"), core.bank(c, D), func)\
                    .then_inc(tile_copied, 1)
            unrolled(act, NB, 4, slot, 4, 4)

        @block.sync
        def _(sp):
            def slot(s, c, t):
                sp.wait_ge(product_used, s + 1)
                store(sp, s, c).then_inc(stored[c], 16)
            unrolled(sp, NB, 4, slot, 4, 4)
            for r in range(4):
                sp.wait_ge(stored[r], 16 * ((NB + 3 - r) // 4))


def row_moments(nc, core, name, steps, rows, load=None, store=None):
    last = len(steps)
    with ExitStack() as st:
        used, counted = sems(nc, st, f"{name}_used {name}_counted")
        loaded, kept = ring_sems(nc, st, f"{name}_loaded", 4), ring_sems(nc, st, f"{name}_kept", 4)
        block = st.enter_context(nc.Block())

        @block.vector
        def _(dve):
            def slot(s, c, t):
                if in_range(s, 0, NB) and load is not None:
                    dve.wait_ge(loaded[c], (t + 1) * 16)
                for n, step in enumerate(steps):
                    if in_range(s, n, NB + n):
                        done = step(s - n, (c - n) % 4)
                        if n == 0:
                            done.then_inc(used, 1)
                if in_range(s, last, NB + last):
                    row_stats(nc, core, s - last, rows(s - last)).then_inc(counted if steps else used, 1)
                if steps:
                    dve.drain()
            unrolled(dve, NB + last, 4, slot, 4, 4)

        @block.sync
        def _(sp):
            def slot(s, c, t):
                if load is not None and in_range(s, 0, NB):
                    ge(sp, used, s - 3)
                    load(sp, s, c).then_inc(loaded[c], 16)
                if store is not None and in_range(s, 4, NB + 4):
                    sp.wait_ge(counted, s - 3)
                    ge(sp, kept[c], (turn(t, c, 4, 4)) * 16)
                    store(sp, s - 4).then_inc(kept[c], 16)
            if load is not None or store is not None:
                unrolled(sp, NB + 4, 4, slot, 8, 4)
            if store is not None:
                for r in range(4):
                    sp.wait_ge(kept[r], 16 * ((NB + 3 - r) // 4))
    finish_moments(nc, core, name)


def row_stats(nc, core, b, rows):
    return nc.vector.bn_stats(core.moments[:, bass.ds(b, 1), 3:9].rearrange("p o n -> p (o n)"), rows)


def finish_moments(nc, core, name):
    with ExitStack() as st:
        moments_set, rooted = sems(nc, st, f"{name}_moments {name}_rooted")
        block = st.enter_context(nc.Block())

        @block.vector
        def _(dve):
            m = core.moments
            half_diff = m[:, :, 9:10]
            nc.vector.tensor_tensor(m[:, :, 0:1], m[:, :, 4:5], m[:, :, 7:8], ALU.add)
            nc.vector.tensor_tensor(half_diff, m[:, :, 4:5], m[:, :, 7:8], ALU.subtract)
            nc.vector.tensor_tensor(m[:, :, 1:2], m[:, :, 5:6], m[:, :, 8:9], ALU.add)
            dve.drain()
            nc.vector.tensor_scalar(m[:, :, 0:1], m[:, :, 0:1], 0.5, None, ALU.mult)
            nc.vector.scalar_tensor_tensor(half_diff, half_diff, 0.25, half_diff, ALU.mult, ALU.mult)
            nc.vector.tensor_scalar(m[:, :, 1:2], m[:, :, 1:2], 1.0 / D, EPS, ALU.mult, ALU.add)
            dve.drain()
            nc.vector.tensor_tensor(m[:, :, 2:3], m[:, :, 1:2], half_diff, ALU.add).then_inc(moments_set, 1)
            dve.wait_ge(rooted, 1)
            nc.vector.reciprocal(core.moments[:, :, 2:3], core.moments[:, :, 1:2])

        @block.scalar
        def _(act):
            act.wait_ge(moments_set, 1)
            nc.scalar.activation(core.moments[:, :, 1:2], core.moments[:, :, 2:3], ACT.Sqrt).then_inc(rooted, 1)


def normalized(nc, core, out, x, b):
    m = core.moments[:, bass.ds(b, 1)].rearrange("p o n -> p (o n)")
    return nc.vector.tensor_scalar(out, x, m[:, 0:1], m[:, 2:3], ALU.subtract, ALU.mult)


def cols(b, width, base=0, n=None):
    return bass.ds(b * width + base, n or width)


def gat1_tables(nc, core, x, w1, al1, ar1, table):
    xs = core.arena[:, 0:NB * D]
    wk = core.hot[:, 0:2, 0:D + 2 * H1]
    rows = core.work[:, 8 * D:8 * D + 4 * ROW1].rearrange("p (r n) -> p r n", r=4)
    add_attention_columns(nc, core, w1, (al1, ar1), H1, wk)
    with nc.Block() as block:
        @block.vector
        def _(dve):
            nc.vector.memset(xs[:, (NB - 1) * D:NB * D], 0.0)
            nc.vector.memset(rows, 1.0)

    def load(sp, s, r):
        n = TAIL if isinstance(s, int) and s == NB - 1 else P
        return sp.dma_start(xs[0:n, cols(s, D)], x[bass.ds(s * P, n), :])

    row_moments(nc, core, "x0", (), lambda s: xs[:, cols(s, D)], load)

    def prepare(dve, s, tile):
        return normalized(nc, core, tile, xs[:, cols(s, D)], s)

    def finish(dve, s, prod, r):
        head = rows[:, r, 0:D + H1].rearrange("p (h c) -> p h c", h=H1)
        nc.vector.tensor_copy(head[:, :, 0:HD], prod[:, 0:D].rearrange("p (h c) -> p h c", h=H1))
        nc.vector.tensor_copy(rows[:, r, D + H1:ROW1], prod[:, D:D + H1])
        nc.vector.tensor_copy(core.el[:, :, bass.ds(s, 1)], prod[:, D:D + H1].unsqueeze(2))
        return nc.vector.tensor_copy(core.er[:, :, bass.ds(s, 1)], prod[:, D + H1:D + 2 * H1].unsqueeze(2))

    def store(sp, s, r):
        return sp.dma_start(table[bass.ds(s * P, P), :], rows[:, r])

    dense_tiles(nc, "g1", core, [wk[:, 0], wk[:, 1]], D + 2 * H1, prepare, finish, store)


def add_attention_columns(nc, core, w, vecs, heads, wk):
    hd = D // heads
    a = core.work[:, 0:2 * D].rearrange("p (v n) -> p v n", v=2)
    prod = core.work[:, 2 * D:4 * D]
    with ExitStack() as st:
        w_in, = sems(nc, st, "w_in")
        block = st.enter_context(nc.Block())

        @block.sync
        def _(sp):
            sp.dma_start(wk[:, :, 0:D], w.rearrange("(k p) n -> p k n", p=P)).then_inc(w_in, 16)
            for v in range(2):
                sp.dma_start(a[:, v], vecs[v].rearrange("h d -> (h d)").partition_broadcast(P)).then_inc(w_in, 16)

        @block.vector
        def _(dve):
            dve.wait_ge(w_in, 48)
            for k in range(2):
                for v in range(2):
                    dve.drain()
                    nc.vector.tensor_tensor(prod[:, 0:D], wk[:, k, 0:D], a[:, v], ALU.mult)
                    dve.drain()
                    nc.vector.tensor_reduce(wk[:, k, D + v * heads:D + (v + 1) * heads],
                                            prod[:, 0:D].rearrange("p (h d) -> p h d", h=heads), AX.X, ALU.add)


def spread_attention(nc, core, heads):
    sb = core.work
    turned = sb[0:NB, 0:heads * P].rearrange("b (h p) -> b h p", h=heads)
    small = sb[:, 1024:1024 + 256]
    with ExitStack() as st:
        min_set, min_turned, min_all, min_spread, er_turned, er_copied, er_spread, er_used = sems(
            nc, st, "min_set min_turned min_all min_spread er_turned er_copied er_spread er_used")
        block = st.enter_context(nc.Block())

        @block.vector
        def _(dve):
            nc.vector.tensor_reduce(small[:, 0:1], core.el[:, 0:heads], AX.XY, ALU.min).then_inc(min_set, 1)
            dve.wait_ge(min_turned, 1)
            nc.vector.tensor_reduce(small[0:1, 1:2], core.bank(0, P)[0:1, :], AX.X, ALU.min).then_inc(min_all, 1)
            dve.wait_ge(min_spread, 1)
            nc.vector.tensor_scalar(core.low[:, 0:1], core.bank(1, 1), -1.0, None, ALU.add)
            nc.vector.tensor_scalar(core.low[:, 1:2], core.bank(1, 1), -1.0, 1.0, ALU.mult, ALU.add)
            dve.wait_ge(er_turned, heads)
            for h in range(heads):
                last = nc.vector.tensor_copy(turned[:, h], core.bank(2, heads * P)[0:NB, h * P:(h + 1) * P])
            last.then_inc(er_copied, 1)
            er, parts = core.er_steps, core.er_parts
            for h in range(heads):
                dve.wait_ge(er_spread, h + 1)
                nc.vector.tensor_copy(core.er_steps[:, h].rearrange("p (a k) -> p a k", a=2),
                                      core.psum[:, 2048 + h * 1024:3072 + h * 1024]
                                      .rearrange("p (a k) -> p a k", a=2)[:, :, 0:SK // 2])
            rest = core.work[:, 2048:2048 + heads * SK].rearrange("p (h k) -> p h k", h=heads)
            dve.drain()
            nc.vector.tensor_copy(parts[:, 0, 0:heads], er[:, 0:heads])
            dve.drain()
            nc.vector.tensor_tensor(rest, er[:, 0:heads], parts[:, 0, 0:heads], ALU.subtract)
            dve.drain()
            nc.vector.tensor_copy(parts[:, 1, 0:heads], rest)
            dve.drain()
            nc.vector.tensor_tensor(parts[:, 2, 0:heads], rest, parts[:, 1, 0:heads], ALU.subtract)

        @block.tensor
        def _(pe):
            pe.wait_ge(min_set, 1)
            nc.tensor.transpose(core.bank(0, P)[0:1, :], small[:, 0:1], core.ident[:]).then_inc(min_turned, 1)
            for h in range(heads):
                nc.tensor.transpose(core.bank(2, heads * P)[0:NB, h * P:(h + 1) * P], core.er[:, h], core.ident[:])\
                    .then_inc(er_turned, 1)
            pe.wait_ge(min_all, 1)
            nc.tensor.matmul(core.bank(1, 1), core.ones[0:1, :], small[0:1, 1:2], start=True, stop=True).then_inc(min_spread, 1)
            pe.wait_ge(er_copied, 1)
            for h in range(heads):
                for a in range(2):
                    last = nc.tensor.matmul(core.bank(4 + 2 * h + a, SK // 2), turned[:, h],
                                            core.step_sel[:, a * (SK // 2):(a + 1) * (SK // 2)], start=True, stop=True)
                last.then_inc(er_spread, 1)


def edge_pass(nc, core, name, table, row, heads, attend):
    G4 = GS * heads
    unit = row // heads if not attend else (D // heads + 1)
    el0 = heads * unit
    ring = core.work[:, 0:RING * GS * row].rearrange("p (r j n) -> p r j n", r=RING, j=GS)
    low = 0

    def take(n):
        nonlocal low
        low += n
        return core.arena[:, low - n:low]

    if attend:
        masked = take(G4 * P).rearrange("p (j h d) -> p j h d", j=GS, h=heads)
        weighted = take(2 * GS * heads * unit).rearrange("p (r j n) -> p r j n", r=2, j=GS)
        pick_t = take(GS * P).bitcast(BF16).rearrange("p (r j e) -> p r j e", r=2, j=GS)
        dl_ring = take(GS * P).bitcast(BF16).rearrange("p (r n) -> p r n", r=2)
        edge = take(10 * G4).rearrange("p (n j h) -> p n j h", n=10, j=GS)
        lift = take(RING * G4).rearrange("p (r j h) -> p r j h", r=RING, j=GS)
        run_max = take(2 * heads * (GS + 1)).rearrange("p (r h j) -> p r h j", r=2, h=heads)
        kept_max = take(2 * heads * (GS + 1)).rearrange("p (r h j) -> p r h j", r=2, h=heads)
        known = take(6 * G4).bitcast(BF16).rearrange("p (r i j n) -> p r i j n", r=2, i=3, j=GS)
        scale = take(RING * G4).rearrange("p (r j h) -> p r j h", r=RING, j=GS)
        top, lifted, slope, drop_a, drop, term, term_s, gap, gap_c, weight = (edge[:, n] for n in range(10))
        assert low <= AGG0
    pick = core.hot[:].rearrange("p r (j d) -> p r j d", j=GS)
    idx_ring = core.idx_ring
    TURNED = 3 - heads
    turned = core.psum[:, 0:TURNED * G4 * P].rearrange("p (r n) -> p r n", r=TURNED)
    at_edge = core.bank(4, GS * 2 * heads).rearrange("p (j n) -> p j n", j=GS)

    sum_banks = (5, 6, 7)

    def sums(j):
        return core.bank(sum_banks[j % len(sum_banks)], heads * unit)

    def bank_back(j):
        back = 1
        while (j - back) % GS % len(sum_banks) != j % len(sum_banks):
            back += 1
        return back

    SLOTS = NG + 2
    HALF = GS // 2
    with ExitStack() as st:
        names = ("idx_set pick_set terms_set masked_set turned_done top_read max_set edge_done gap_set "
                 "weight_set scale_set dl_free weighted_set lifted_set slope_set run_set part_set kept_set drop_set "
                 "fall_set term_set score_set edge_read").split()
        (idx_set, pick_set, terms_set, masked_set, turned_done, top_read, max_set, edge_done, gap_set,
         weight_set, scale_set, dl_free, weighted_set, lifted_set, slope_set, run_set, part_set, kept_set,
         drop_set, fall_set, term_set, score_set, edge_read) = sems(
            nc, st, " ".join(f"{name}_{x}" for x in names))
        rows_in = [core.stack.enter_context(nc.semaphore(f"{name}_rows_in{r}")) for r in range(RING)]
        sums_done = ring_sems(nc, st, f"{name}_sums_done", GS)
        added = ring_sems(nc, st, f"{name}_added", GS)
        dl_in = ring_sems(nc, st, f"{name}_dl_in", 2)
        block = st.enter_context(nc.Block())

        @block.gpsimd
        def _(pool):
            def slot(s, c, t):
                pool.wait_ge(idx_set, s + 1)
                for j in range(GS):
                    if attend and j % 2 == 0:
                        ge(pool, weighted_set, HALF * (s - RING) + j // 2 + 1)
                        pool.nop(nofuse=True)
                    elif not attend and j == 0:
                        ge(pool, sums_done[GS - 1], s - RING + 1)
                        pool.nop(nofuse=True)
                    nc.gpsimd.indirect_dma_start(
                        ring[:, c, j], None, table,
                        bass.IndirectOffsetOnAxis(ap=idx_ring[:, c, j:j + 1], axis=0)).then_inc(rows_in[c], 16)
            unrolled(pool, NG, RING, slot, 4, 2)

        if attend:
            @block.sync
            def _(sp):
                def slot(s, c, t):
                    ge(sp, dl_free, s - 1)
                    sp.dma_start(dl_ring[:, c % 2],
                                 core.dl_rows.rearrange("k e -> (k e)")[cols(s, GS * P)].partition_broadcast(P))\
                        .then_inc(dl_in[c % 2], 16)
                unrolled(sp, NG, RING, slot, 4, 2)

        @block.vector
        def _(dve):
            def select(g, q, t):
                ge(dve, sums_done[GS - 1], g - RING + 1)
                nc.vector.tensor_tensor(
                    pick[:, q], core.iota_col[:].unsqueeze(1).to_broadcast([P, GS, P]),
                    core.step_dst[:, cols(g, GS)].unsqueeze(2).to_broadcast([P, GS, P]), ALU.is_equal)\
                    .then_inc(pick_set, 1)

            def raise_terms(g, q, t):
                dve.wait_ge(rows_in[q], (t + 1) * 16 * GS)
                ge(dve, masked_set, 2 * (g - RING + 1))
                nc.vector.tensor_scalar(lift[:, q], ring[:, q, :, el0:el0 + heads], core.low[:, 1:2], None, ALU.add)\
                    .then_inc(terms_set, 1)

            def slot(s, c, t):
                new, mid, old = in_range(s, 0, NG - 1), in_range(s, 1, NG + 1), in_range(s, 2, SLOTS)
                r = (c + 1) % 2
                gm, go = s - 1, s - 2
                same = core.step_same[:, cols(go, GS)] if old else None
                at = []

                def load_places():
                    if old:
                        at.extend(nc.values_load_multi_w_load_instructions(
                            core.step_at[0:1, cols(go, GS)], engines=[mybir.EngineType.DVE], min_val=AGG0,
                            max_val=ARENA - ACW,
                            skip_runtime_bounds_check_because="a step's block is a count of at most NB - 1 starts")[1])

                def add(j):
                    if not old:
                        return
                    dve.wait_ge(sums_done[j], go + 1)
                    if attend and j == 0:
                        dve.wait_ge(scale_set, s - 1)
                    for h in range(heads):
                        ge(dve, added[(j - 1) % GS], (go if j else go - 1) * heads + h + 1)
                        own = core.arena[:, h * unit:ARENA - ACW + D + H1][:, bass.ds(at[j], unit)]
                        keep = scale[:, (c - 2) % RING, j, h:h + 1] if attend else same[:, j:j + 1]
                        nc.vector.scalar_tensor_tensor(own, own, keep, sums(j)[:, h * unit:(h + 1) * unit],
                                                       ALU.mult, ALU.add).then_inc(added[j], 1)

                if not attend:
                    load_places()
                    for j in range(GS):
                        add(j)
                    if new:
                        select(s + 1, (c + 1) % RING, turn(t, c, -1, RING))
                    return
                if mid:
                    for a in range(2):
                        dve.wait_ge(turned_done, 2 * (s - 1) + a + 1)
                        nc.vector.tensor_reduce(
                            top.rearrange("p j h -> p (j h)")[:, a * (G4 // 2):(a + 1) * (G4 // 2)],
                            turned[:, (c - 1) % TURNED].rearrange("p (a n e) -> p a n e", a=2, e=P)[:, a], AX.X, ALU.max).then_inc(top_read, 1)
                    ge(dve, edge_done, s - 2)
                    nc.vector.tensor_copy(known[:, r, :, :, 0:heads].rearrange("p i j h -> p i h j"),
                                          core.er_parts[:, :, 0:heads, cols(gm, GS)])
                    nc.vector.tensor_copy(kept_max[:, r, :, 0:1], kept_max[:, 1 - r, :, GS:GS + 1])
                    dve.wait_ge(top_read, 2 * s)
                    nc.vector.scalar_tensor_tensor(
                        lifted, top, core.low[:, 0:1], core.er_steps[:, 0:heads, cols(gm, GS)].rearrange("p h j -> p j h"),
                        ALU.add, ALU.add).then_inc(lifted_set, 1)
                if new:
                    select(s + 1, (c + 1) % RING, turn(t, c, -1, RING))
                load_places()
                if mid:
                    dve.wait_ge(lifted_set, s)
                    nc.vector.scalar_tensor_tensor(slope, lifted, SLOPE, lifted, ALU.mult, ALU.max)\
                        .then_inc(slope_set, 1)
                if in_range(s, 0, NG):
                    dve.wait_ge(dl_in[c % 2], (t * (RING // 2) + c // 2 + 1) * 16)
                    ge(dve, edge_done, s - 1)
                    nc.vector.tensor_scalar(pick_t[:, c % 2].rearrange("p j e -> p (j e)"), dl_ring[:, c % 2],
                                            core.part[:, 0:1], None, ALU.is_equal).then_inc(dl_free, 1)
                if mid:
                    reset = core.step_reset[:, cols(gm, GS)]
                    now = run_max[:, r, :, 1:GS + 1]
                    part = [known[:, r, i, :, heads:2 * heads].rearrange("p j h -> p h j") for i in range(2)]
                    dve.wait_ge(slope_set, s)
                    for h in range(heads):
                        nc.vector.tensor_tensor_scan(run_max[:, r, h, 1:GS + 1], reset, slope[:, :, h],
                                                     run_max[:, 1 - r, h, GS:GS + 1], ALU.add, ALU.max)\
                            .then_inc(run_set, 1)
                if new:
                    raise_terms(s + 1, (c + 1) % RING, turn(t, c, -1, RING))
                add(0)
                if mid:
                    dve.wait_ge(run_set, s * heads)
                    nc.vector.tensor_copy(part[0], now).then_inc(part_set, 1)
                if mid:
                    dve.wait_ge(part_set, s)
                    nc.vector.tensor_tensor(part[1], now, part[0], ALU.subtract).then_inc(max_set, 1)
                add(1)
                if mid:
                    dve.wait_ge(max_set, s)
                    nc.vector.tensor_tensor(kept_max[:, r, :, 1:GS + 1], part[0], part[1], ALU.add)\
                        .then_inc(kept_set, 1)
                add(2)
                if mid:
                    dve.wait_ge(kept_set, s)
                    nc.vector.tensor_tensor(drop_a.rearrange("p j h -> p h j"), kept_max[:, r, :, 0:GS],
                                            reset.unsqueeze(1).to_broadcast([P, heads, GS]), ALU.add)\
                        .then_inc(drop_set, 1)
                add(3)
                if mid:
                    dve.wait_ge(drop_set, s)
                    ge(dve, scale_set, s - 1)
                    nc.vector.tensor_tensor(drop.rearrange("p j h -> p h j"), drop_a.rearrange("p j h -> p h j"),
                                            kept_max[:, r, :, 1:GS + 1], ALU.subtract).then_inc(fall_set, 1)
                    dve.wait_ge(edge_done, s)
                    nc.vector.tensor_tensor(term, ring[:, (c - 1) % RING, :, el0:el0 + heads],
                                            at_edge[:, :, 0:heads], ALU.add).then_inc(term_set, 1)
                add(4)
                if mid:
                    dve.wait_ge(term_set, s)
                    nc.vector.scalar_tensor_tensor(term_s, term, SLOPE, term, ALU.mult, ALU.max)\
                        .then_inc(score_set, 1)
                add(5)
                if mid:
                    dve.wait_ge(score_set, s)
                    nc.vector.tensor_tensor(gap, term_s, at_edge[:, :, heads:2 * heads], ALU.subtract)\
                        .then_inc(edge_read, 1)
                add(6)
                if mid:
                    dve.wait_ge(edge_read, s)
                    ge(dve, weight_set, s - 1)
                    nc.vector.tensor_scalar(gap_c, gap, 30.0, None, ALU.min).then_inc(gap_set, 1)
                add(7)

            if attend:
                nc.vector.memset(run_max, 0.0)
                nc.vector.memset(kept_max, 0.0)
                nc.vector.memset(known, 0.0)
                dve.drain()
            select(0, 0, 0)
            if attend:
                raise_terms(0, 0, 0)
            unrolled(dve, SLOTS, RING, slot, 4, 4)

        @block.tensor
        def _(pe):
            def flip(g, c):
                for j in range(GS):
                    if j % HALF == 0:
                        pe.wait_ge(masked_set, 2 * g + j // HALF + 1)
                        ge(pe, top_read, 2 * (g - TURNED) + j // HALF + 1)
                    for h in range(heads):
                        n = j * heads + h
                        last = nc.tensor.transpose(turned[:, c % TURNED, n * P:(n + 1) * P], masked[:, j, h], core.ident[:])
                    if j % HALF == HALF - 1:
                        last.then_inc(turned_done, 1)

            def slot(s, c, t):
                mid, old = in_range(s, 1, NG + 1), in_range(s, 2, SLOTS)
                go = s - 2

                def sum_step(j):
                    back = j - bank_back(j)
                    ge(pe, added[back % GS], (go + 1 if back >= 0 else go) * heads)
                    rhs = weighted[:, c % 2, j] if attend else ring[:, (c - 2) % RING, j, 0:unit]
                    if attend and j % 2 == 0:
                        pe.wait_ge(weighted_set, HALF * go + j // 2 + 1)
                    nc.tensor.matmul(sums(j), pick[:, (c - 2) % RING, j], rhs, start=True, stop=True)\
                        .then_inc(sums_done[j], 1)

                if not attend:
                    if old:
                        pe.wait_ge(pick_set, s - 1)
                        pe.wait_ge(rows_in[(c - 2) % RING], (turn(t, c, 2, RING) + 1) * 16 * GS)
                        for j in range(GS):
                            sum_step(j)
                    return
                if TURNED == 1 and in_range(s, 0, NG):
                    flip(s, c)
                if old:
                    for j in range(3):
                        sum_step(j)
                if mid:
                    pe.wait_ge(max_set, s)
                    pe.wait_ge(dl_free, s)
                    ge(pe, edge_read, s - 1)
                    for j in range(GS):
                        for i in range(3):
                            last = nc.tensor.matmul(at_edge[:, j], pick_t[:, (c + 1) % 2, j],
                                                    known[:, (c + 1) % 2, i, j], start=(i == 0), stop=(i == 2))
                    last.then_inc(edge_done, 1)
                if old:
                    for j in range(3, GS):
                        sum_step(j)
                if TURNED == 2 and in_range(s, 0, NG - 1):
                    flip(s + 1, c + 1)
            if attend and TURNED == 2:
                flip(0, 0)
            unrolled(pe, SLOTS, RING, slot, 4, 4)

        @block.scalar
        def _(act):
            def stage(g, q):
                nc.scalar.copy(idx_ring[:, q], core.step_idx[:, cols(g, GS)]).then_inc(idx_set, 1)

            def mask(g, q):
                act.wait_ge(pick_set, g + 1)
                act.wait_ge(terms_set, g + 1)
                for j in range(GS):
                    if j % HALF == 0:
                        ge(act, turned_done, 2 * (g - 1) + j // HALF + 1)
                    for h in range(heads):
                        last = nc.scalar.activation(masked[:, j, h], pick[:, q, j], ACT.Copy, scale=lift[:, q, j, h:h + 1])
                    if j % HALF == HALF - 1:
                        last.then_inc(masked_set, 1)

            def slot(s, c, t):
                if in_range(s, 0, NG - 2):
                    ge(act, rows_in[(c + 3) % RING], turn(t, c, -3, RING) * 16 * GS)
                    stage(s + 3, (c + 3) % RING)
                if not attend:
                    return
                if in_range(s, 2, NG + 2):
                    go, r = s - 2, c % 2
                    act.wait_ge(gap_set, s - 1)
                    ge(act, weighted_set, HALF * go)
                    nc.scalar.activation(weight, gap_c, ACT.Exp).then_inc(weight_set, 1)
                    act.wait_ge(weight_set, s - 1)
                    ge(act, sums_done[GS - 1], go - 1)
                    for j in range(GS):
                        for h in range(heads):
                            last = nc.scalar.activation(weighted[:, r, j, h * unit:(h + 1) * unit],
                                                        ring[:, (c - 2) % RING, j, h * unit:(h + 1) * unit],
                                                        ACT.Copy, scale=weight[:, j, h:h + 1])
                        if j % 2 == 1:
                            last.then_inc(weighted_set, 1)
                if in_range(s, 0, NG - 1):
                    mask(s + 1, (c + 1) % RING)
                if in_range(s, 1, NG + 1):
                    act.wait_ge(fall_set, s)
                    ge(act, added[GS - 1], (s - RING) * heads)
                    nc.scalar.activation(scale[:, (c - 1) % RING], drop, ACT.Exp).then_inc(scale_set, 1)
            for g in range(3):
                stage(g, g)
            if attend:
                mask(0, 0)
            unrolled(act, SLOTS if attend else NG, RING, slot, 8, 4)


def gat2_tables(nc, core, w2, al2, ar2, b1, table):
    wk = core.hot[:, 0:2, 0:D + 2]
    bias = core.hot[:, 2, 0:D]
    inv = core.hot[:, 3, 0:NB * H1].rearrange("p (b h) -> p b h", b=NB)
    rows = core.work[:, 8 * D:8 * D + 4 * ROW2].rearrange("p (r n) -> p r n", r=4)
    add_attention_columns(nc, core, w2, (al2, ar2), 1, wk)
    weight_sums(nc, core, "s1", H1, inv, b1, bias, rows)

    def prepare(dve, s, tile):
        for h in range(H1):
            last = nc.vector.scalar_tensor_tensor(
                tile[:, h * HD:(h + 1) * HD], core.arena[:, cols(s, ACW, AGG0 + h * (HD + 1), HD)],
                inv[:, bass.ds(s, 1), h:h + 1].rearrange("p o n -> p (o n)"), bias[:, h * HD:(h + 1) * HD],
                ALU.mult, ALU.add)
        return last

    def finish(dve, s, prod, r):
        nc.vector.tensor_copy(rows[:, r, 0:D], prod[:, 0:D])
        nc.vector.tensor_copy(rows[:, r, D + 1:ROW2], prod[:, D:D + 1])
        nc.vector.tensor_copy(core.el[:, 0:1, bass.ds(s, 1)], prod[:, D:D + 1].unsqueeze(2))
        return nc.vector.tensor_copy(core.er[:, 0:1, bass.ds(s, 1)], prod[:, D + 1:D + 2].unsqueeze(2))

    def store(sp, s, r):
        return sp.dma_start(table[bass.ds(s * P, P), :], rows[:, r])

    dense_tiles(nc, "g2", core, [wk[:, 0], wk[:, 1]], D + 2, prepare, finish, store, func=ACT.Relu)


def weight_sums(nc, core, name, heads, inv, vec, bias, rows=None):
    unit = D // heads
    agg = core.arena[:, AGG0:ARENA].rearrange("p (b n) -> p b n", b=NB)
    sums = agg[:, :, 0:heads * (unit + 1)].rearrange("p b (h c) -> p b h c", h=heads)[:, :, :, unit]
    with ExitStack() as st:
        vec_in, = sems(nc, st, f"{name}_vec_in")
        block = st.enter_context(nc.Block())

        @block.sync
        def _(sp):
            sp.dma_start(bias, vec.rearrange("h d -> (h d)").partition_broadcast(P)).then_inc(vec_in, 16)
            sp.wait_ge(vec_in, 16)

        @block.vector
        def _(dve):
            if rows is not None:
                nc.vector.memset(rows, 1.0)
            nc.vector.tensor_scalar(inv, sums, 1.0e-30, None, ALU.max)
            dve.drain()
            nc.vector.reciprocal(inv, inv)


def first_residual(nc, core, x, b2, x1_rows):
    inv = core.hot[:, 3, 0:NB].rearrange("p (b h) -> p b h", b=NB)
    bias = core.hot[:, 2, 0:D]
    x_ring = core.work[:, 0:4 * D].rearrange("p (r n) -> p r n", r=4)
    weight_sums(nc, core, "s2", 1, inv, b2, bias)

    def place(s):
        return core.arena[:, cols(s, ACW, AGG0, D)]

    def own_part(s, r):
        return nc.vector.scalar_tensor_tensor(place(s), place(s), inv[:, bass.ds(s, 1), 0:1].rearrange("p o n -> p (o n)"),
                                              x_ring[:, r], ALU.mult, ALU.add)

    def add_bias(s, r):
        return nc.vector.tensor_tensor(place(s), place(s), bias, ALU.add)

    def load(sp, s, r):
        n = TAIL if isinstance(s, int) and s == NB - 1 else P
        return sp.dma_start(x_ring[0:n, r], x[bass.ds(s * P, n), :])

    def store(sp, s):
        return sp.dma_start(x1_rows[bass.ds(s * P, P), :], place(s))

    row_moments(nc, core, "x1", (own_part, add_bias), place, load, store)


def slice_logits(nc, core, w_xt, b_x, w_slice, b_slice, temp, wl, bl):
    HC = NH * NSL
    wx = core.work[0:DH, 0:NH * D].rearrange("c (h k) -> c h k", h=NH)
    ws = core.work[0:DH, 2048:2048 + NSL]
    bx = core.work[0:DH, 2112:2112 + NH]
    bx_wide = core.work[0:DH, 2120:2120 + NH * P].rearrange("c (h p) -> c h p", h=NH)
    bs = core.work[:, 3200:3200 + NSL]
    inv_t = core.work[:, 3264:3264 + NH]
    biased = core.work[:, 3300:3300 + HC].rearrange("p (h g) -> p h g", h=NH)
    with ExitStack() as st:
        weights_in, bias_wide_set, maps_done = sems(nc, st, "weights_in bias_wide_set maps_done")
        block = st.enter_context(nc.Block())

        @block.sync
        def _(sp):
            for t, a in ((wx, w_xt.rearrange("(h c) k -> c h k", h=NH)), (ws, w_slice),
                         (bx, b_x), (bs, b_slice.partition_broadcast(P)),
                         (inv_t, temp.partition_broadcast(P))):
                sp.dma_start(t, a).then_inc(weights_in, 16)

        @block.tensor
        def _(pe):
            pe.wait_ge(weights_in, 80)
            for k in range(2):
                for h in range(NH):
                    nc.tensor.matmul(core.bank(k)[:, h * NSL:(h + 1) * NSL], wx[:, h, k * P:(k + 1) * P], ws,
                                     start=True, stop=True)
            pe.wait_ge(bias_wide_set, 1)
            for h in range(NH):
                last = nc.tensor.matmul(core.bank(2)[:, h * NSL:(h + 1) * NSL], bx_wide[:, h], ws, start=True, stop=True)
            last.then_inc(maps_done, 1)

        @block.vector
        def _(dve):
            dve.wait_ge(weights_in, 80)
            nc.vector.tensor_copy(bx_wide, bx.unsqueeze(2).to_broadcast([DH, NH, P])).then_inc(bias_wide_set, 1)
            nc.vector.tensor_scalar(inv_t, inv_t, 0.1, 5.0, ALU.max, ALU.min)
            dve.drain()
            nc.vector.reciprocal(inv_t, inv_t)
            dve.drain()
            dve.wait_ge(maps_done, 1)
            wide = inv_t.unsqueeze(2).to_broadcast([P, NH, NSL])
            for k in range(2):
                nc.vector.tensor_tensor(wl[:, k].rearrange("p (h g) -> p h g", h=NH),
                                        core.bank(k).rearrange("p (h g) -> p h g", h=NH), wide, ALU.mult)
            nc.vector.tensor_tensor(biased, core.bank(2).rearrange("p (h g) -> p h g", h=NH),
                                    bs.unsqueeze(1).to_broadcast([P, NH, NSL]), ALU.add)
            dve.drain()
            nc.vector.tensor_tensor(bl.rearrange("p (h g) -> p h g", h=NH), biased, wide, ALU.mult)


def slice_weights(nc, core, wl, bl):
    HC = NH * NSL
    RINGX = 6
    xl = core.work[:, 5632:5632 + RINGX * D].rearrange("p (r n) -> p r n", r=RINGX)
    xlt = core.work[:, 4 * D:6 * D].rearrange("p (r n) -> p r n", r=2)
    logits = core.work[:, 1536:1536 + 2 * HC].rearrange("p (r n) -> p r n", r=2)
    expd = core.work[:, 2560:2560 + 2 * HC].rearrange("p (r n) -> p r n", r=2)
    sw = core.work[:, 3584:3584 + 2 * HC].rearrange("p (r n) -> p r n", r=2)
    total = core.work[:, 4608:4608 + HC]
    high, weight_sum, inv = (core.work[:, 5120 + 8 * n:5128 + 8 * n] for n in range(3))

    def by_head(t):
        return t.rearrange("p (h g) -> p h g", h=NH)

    def wide(t):
        return t.unsqueeze(2).to_broadcast([P, NH, NSL])

    SLOTS = NB + 4
    with ExitStack() as st:
        (tile_set, tile_turned, tile_copied, product, biased, shifted, exp_set, sw_set, sw_turned, swt_copied,
         tokens_done, totalled) = sems(nc, st, "tile_set tile_turned tile_copied product biased shifted exp_set sw_set "
                                               "sw_turned swt_copied tokens_done totalled")
        block = st.enter_context(nc.Block())

        @block.vector
        def _(dve):
            def slot(s, c, t):
                new, mid, old = in_range(s, 0, NB), in_range(s, 2, NB + 2), in_range(s, 3, NB + 3)
                m, o = c % 2, (c + 1) % 2
                if new:
                    ge(dve, tokens_done, s - RINGX + 1)
                    normalized(nc, core, xl[:, c], core.arena[:, cols(s, ACW, AGG0, D)], s).then_inc(tile_set, 1)
                if mid:
                    dve.wait_ge(product, s - 1)
                    nc.vector.tensor_tensor(logits[:, m], core.bank(2 + m), bl, ALU.add).then_inc(biased, 1)
                if old:
                    dve.wait_ge(exp_set, s - 2)
                    nc.vector.tensor_reduce(weight_sum, by_head(expd[:, o]), AX.X, ALU.add)
                dve.drain()
                if mid:
                    nc.vector.tensor_reduce(high, by_head(logits[:, m]), AX.X, ALU.max)
                if old:
                    nc.vector.reciprocal(inv, weight_sum)
                dve.drain()
                if mid:
                    nc.vector.tensor_tensor(by_head(expd[:, m]), by_head(logits[:, m]), wide(high), ALU.subtract)\
                        .then_inc(shifted, 1)
                if old:
                    ge(dve, tokens_done, s - 4)
                    ge(dve, totalled, s - 3)
                    nc.vector.tensor_tensor(by_head(sw[:, o]), by_head(expd[:, o]), wide(inv), ALU.mult)\
                        .then_inc(sw_set, 1)
            unrolled(dve, NB + 3, RINGX, slot, RINGX, 4)

        @block.scalar
        def _(act):
            def slot(s, c, t):
                if in_range(s, 0, NB):
                    act.wait_ge(tile_turned, s + 1)
                    ge(act, product, s - 1)
                    nc.scalar.activation(xlt[:, c % 2], core.bank(c % 2, D), ACT.Copy).then_inc(tile_copied, 1)
                if in_range(s, 2, NB + 2):
                    act.wait_ge(shifted, s - 1)
                    nc.scalar.activation(expd[:, c % 2], expd[:, c % 2], ACT.Exp).then_inc(exp_set, 1)
                if in_range(s, 4, SLOTS):
                    act.wait_ge(sw_turned, s - 3)
                    nc.scalar.activation(core.arena[:, cols(s - 4, HC)], core.bank(6 + c % 2), ACT.Copy)\
                        .then_inc(swt_copied, 1)
            unrolled(act, SLOTS, RINGX, slot, RINGX, 5)

        @block.gpsimd
        def _(pool):
            nc.gpsimd.memset(total, 0.0).then_inc(totalled, 1)

            def slot(s, c, t):
                pool.wait_ge(totalled, s + 1)
                pool.wait_ge(sw_set, s + 1)
                rows = TAIL if isinstance(s, int) and s == NB - 1 else P
                nc.gpsimd.tensor_tensor(total[0:rows], total[0:rows], sw[0:rows, c % 2], ALU.add).then_inc(totalled, 1)
            unrolled(pool, NB, 2, slot, 2, 2)

        @block.tensor
        def _(pe):
            def slot(s, c, t):
                if in_range(s, 0, NB):
                    pe.wait_ge(tile_set, s + 1)
                    ge(pe, tile_copied, s - 1)
                    for k in range(2):
                        last = nc.tensor.transpose(core.bank(c % 2)[:, k * P:(k + 1) * P], xl[:, c, k * P:(k + 1) * P],
                                                   core.ident[:])
                    last.then_inc(tile_turned, 1)
                if in_range(s, 4, SLOTS):
                    r = c % 2
                    rows = TAIL if isinstance(s, int) and s == SLOTS - 1 else P
                    pe.wait_ge(sw_set, s - 3)
                    ge(pe, swt_copied, s - 5)
                    for q in range(4):
                        last = nc.tensor.transpose(core.bank(6 + r)[:, q * P:(q + 1) * P], sw[:, r, q * P:(q + 1) * P],
                                                   core.ident[:])
                    last.then_inc(sw_turned, 1)
                    for k in range(2):
                        last = nc.tensor.matmul(core.bank(4 + k), xl[0:rows, (c - 4) % RINGX, k * P:(k + 1) * P],
                                                sw[0:rows, r], start=isinstance(s, int) and s == 4,
                                                stop=isinstance(s, int) and s == SLOTS - 1)
                    last.then_inc(tokens_done, 1)
                if in_range(s, 1, NB + 1):
                    pe.wait_ge(tile_copied, s)
                    ge(pe, biased, s - 2)
                    for k in range(2):
                        last = nc.tensor.matmul(core.bank(2 + (c + 1) % 2), xlt[:, (c + 1) % 2, k * P:(k + 1) * P],
                                                wl[:, k], start=(k == 0), stop=(k == 1))
                    last.then_inc(product, 1)
            unrolled(pe, SLOTS, RINGX, slot, RINGX, 5)
    return total


def slice_attention(nc, core, total, w_fx, b_fx, w_q, w_k, w_v, w_out, v2):
    HC = NH * NSL
    at = [0]

    def scratch(n, parts=P):
        at[0] += n
        return core.work[0:parts, at[0] - n:at[0]]

    fx = scratch(2 * INNER).rearrange("p (k n) -> p k n", k=2)
    out_w = scratch(NH * D, DH).rearrange("c (h n) -> c h n", h=NH)
    sums = scratch(2 * HC).rearrange("p (k n) -> p k n", k=2)
    at[0] += HC
    assert at[0] == 4608
    at[0] += HC
    norm, inv_norm = scratch(HC, DH), scratch(HC, DH)
    token, qt, kt, v = (scratch(HC, DH) for _ in range(4))
    attn, attn_t, out_t = (scratch(HC, DH) for _ in range(3)) if at[0] + 3 * HC <= 8320 else (None,) * 3
    if attn is None:
        attn, attn_t, out_t = (core.hot[0:DH, 3, 0:HC], core.hot[0:DH, 3, HC:2 * HC], core.hot[0:DH, 2, 0:HC])
    qkv = core.hot[0:DH, 2, HC:HC + 3 * DH].rearrange("p (i n) -> p i n", i=3)
    bfx = core.hot[0:DH, 2, 800:800 + NH]
    high, weight_sum, inv = (core.hot[0:DH, 2, 808 + 8 * n:816 + 8 * n] for n in range(3))

    def by_head(t):
        return t.rearrange("p (h g) -> p h g", h=NH)

    def wide(t):
        return t.unsqueeze(2).to_broadcast([DH, NH, NSL])

    def head(t, h):
        return t[:, h * NSL:(h + 1) * NSL]

    with ExitStack() as st:
        (loaded, norm_done, sums_copied, maps_done, token_set, qkv_done, qkv_copied, scores_done, shifted, exp_set,
         attn_set, attn_turned, attn_copied, out_done, out_copied, v2_done) = sems(
            nc, st, "sl_loaded norm_done sums_copied maps_done token_set qkv_done qkv_copied scores_done sl_shifted "
                    "sl_exp_set attn_set attn_turned attn_copied out_done out_copied v2_done")
        block = st.enter_context(nc.Block())

        @block.sync
        def _(sp):
            for t, a in ((fx, w_fx.rearrange("(k p) n -> p k n", p=P)), (bfx, b_fx), (qkv[:, 0], w_q), (qkv[:, 1], w_k),
                         (qkv[:, 2], w_v), (out_w, w_out.rearrange("(h c) n -> c h n", h=NH))):
                sp.dma_start(t, a).then_inc(loaded, 16)

        @block.tensor
        def _(pe):
            nc.tensor.matmul(core.bank(0)[0:DH, :], core.ones[:, 0:DH], total, start=True, stop=True).then_inc(norm_done, 1)
            pe.wait_ge(loaded, 96)
            pe.wait_ge(sums_copied, 1)
            for h in range(NH):
                for k in range(2):
                    last = nc.tensor.matmul(head(core.bank(1)[0:DH], h), head(fx[:, k], h), head(sums[:, k], h),
                                            start=(k == 0), stop=(k == 1))
            last.then_inc(maps_done, 1)
            pe.wait_ge(token_set, 1)
            nc.tensor.matmul(core.bank(2)[0:DH], qkv[:, 0], token, start=True, stop=True)
            nc.tensor.matmul(core.bank(3)[0:DH], qkv[:, 1], token, start=True, stop=True)
            for h in range(NH):
                last = nc.tensor.matmul(head(core.bank(4)[0:DH], h), head(token, h), qkv[:, 2], start=True, stop=True)
            last.then_inc(qkv_done, 1)
            pe.wait_ge(qkv_copied, 1)
            for h in range(NH):
                last = nc.tensor.matmul(head(core.bank(5)[0:DH], h), head(qt, h), head(kt, h), start=True, stop=True)
            last.then_inc(scores_done, 1)
            pe.wait_ge(attn_set, 1)
            for h in range(NH):
                last = nc.tensor.transpose(head(core.bank(6)[0:DH], h), head(attn, h), core.ident[0:DH, 0:DH])
            last.then_inc(attn_turned, 1)
            pe.wait_ge(attn_copied, 1)
            for h in range(NH):
                last = nc.tensor.matmul(head(core.bank(7)[0:DH], h), head(v, h), head(attn_t, h), start=True, stop=True)
            last.then_inc(out_done, 1)
            pe.wait_ge(out_copied, 1)
            for j in range(NH // 2):
                for i in range(2):
                    last = nc.tensor.matmul(core.bank(j)[:, i * D:(i + 1) * D], out_t[:, j * P:(j + 1) * P],
                                            out_w[:, 2 * j + i], start=True, stop=True)
            last.then_inc(v2_done, 1)

        @block.vector
        def _(dve):
            for k in range(2):
                last = nc.vector.tensor_copy(sums[:, k], core.bank(4 + k))
            last.then_inc(sums_copied, 1)
            dve.wait_ge(norm_done, 1)
            nc.vector.tensor_copy(norm, core.bank(0)[0:DH])
            nc.vector.tensor_scalar(inv_norm, core.bank(0)[0:DH], EPS, None, ALU.add)
            dve.wait_ge(loaded, 96)
            dve.drain()
            nc.vector.reciprocal(inv_norm, inv_norm)
            nc.vector.tensor_tensor(by_head(norm), by_head(norm), wide(bfx), ALU.mult)
            dve.drain()
            dve.wait_ge(maps_done, 1)
            nc.vector.tensor_tensor(norm, norm, core.bank(1)[0:DH], ALU.add)
            dve.drain()
            nc.vector.tensor_tensor(token, norm, inv_norm, ALU.mult).then_inc(token_set, 1)
            dve.wait_ge(qkv_done, 1)
            for i, t in enumerate((qt, kt, v)):
                last = nc.vector.tensor_copy(t, core.bank(2 + i)[0:DH])
            last.then_inc(qkv_copied, 1)
            dve.wait_ge(scores_done, 1)
            nc.vector.tensor_reduce(high, by_head(core.bank(5)[0:DH]), AX.X, ALU.max)
            dve.drain()
            nc.vector.tensor_tensor(by_head(attn), by_head(core.bank(5)[0:DH]), wide(high), ALU.subtract).then_inc(shifted, 1)
            dve.wait_ge(exp_set, 1)
            nc.vector.tensor_reduce(weight_sum, by_head(attn), AX.X, ALU.add)
            dve.drain()
            nc.vector.reciprocal(inv, weight_sum)
            dve.drain()
            nc.vector.tensor_tensor(by_head(attn), by_head(attn), wide(inv), ALU.mult).then_inc(attn_set, 1)
            dve.wait_ge(attn_turned, 1)
            nc.vector.tensor_copy(attn_t, core.bank(6)[0:DH]).then_inc(attn_copied, 1)
            dve.wait_ge(out_done, 1)
            nc.vector.tensor_copy(out_t, core.bank(7)[0:DH]).then_inc(out_copied, 1)
            dve.wait_ge(v2_done, 1)
            for j in range(NH // 2):
                for i in range(2):
                    nc.vector.tensor_copy(v2[i * DH:(i + 1) * DH, j], core.bank(j)[i * DH:(i + 1) * DH, i * D:(i + 1) * D])

        @block.scalar
        def _(act):
            act.wait_ge(shifted, 1)
            nc.scalar.activation(attn, attn, ACT.Exp, scale=float(DH) ** -0.5).then_inc(exp_set, 1)


def second_residual(nc, core, v2, b_out, x1_rows, x2_rows):
    HC = NH * NSL
    bias = core.hot[:, 2, 0:D]
    x_ring = core.work[:, 0:4 * D].rearrange("p (r n) -> p r n", r=4)
    part_ring = core.work[:, 4 * D:8 * D].rearrange("p (r n) -> p r n", r=4)
    swt = core.work[:, 8 * D:8 * D + 2 * HC].rearrange("p (r q n) -> p r q n", r=2, q=4)
    with ExitStack() as st:
        bias_in, swt_copied, product, biased, x2_set, = sems(nc, st, "bias_in swt2_copied product2 biased2 x2_set")
        x_in, kept = ring_sems(nc, st, "x1_in", 4), ring_sems(nc, st, "x2_kept", 4)
        block = st.enter_context(nc.Block())

        @block.sync
        def _(sp):
            sp.dma_start(bias, b_out.partition_broadcast(P)).then_inc(bias_in, 16)

            def slot(s, c, t):
                if in_range(s, 0, NB):
                    ge(sp, x2_set, s - 3)
                    sp.dma_start(x_ring[:, c], x1_rows[bass.ds(s * P, P), :]).then_inc(x_in[c], 16)
                if in_range(s, 4, NB + 4):
                    sp.wait_ge(x2_set, s - 3)
                    ge(sp, kept[c], turn(t, c, 4, 4) * 16)
                    sp.dma_start(x2_rows[bass.ds((s - 4) * P, P), :], core.arena[:, cols(s - 4, D)]).then_inc(kept[c], 16)
            unrolled(sp, NB + 4, 4, slot, 8, 4)
            for r in range(4):
                sp.wait_ge(kept[r], 16 * ((NB + 3 - r) // 4))

        @block.scalar
        def _(act):
            def slot(s, c, t):
                ge(act, product, s - 1)
                nc.scalar.activation(swt[:, c % 2].rearrange("p q n -> p (q n)"), core.arena[:, cols(s, HC)], ACT.Copy)\
                    .then_inc(swt_copied, 1)
            unrolled(act, NB, 2, slot, 2, 2)

        @block.tensor
        def _(pe):
            def slot(s, c, t):
                pe.wait_ge(swt_copied, s + 1)
                ge(pe, biased, s - 1)
                for q in range(4):
                    last = nc.tensor.matmul(core.bank(c % 2, D), swt[:, c % 2, q], v2[:, q], start=(q == 0), stop=(q == 3))
                last.then_inc(product, 1)
            unrolled(pe, NB, 2, slot, 2, 2)

        @block.vector
        def _(dve):
            dve.wait_ge(bias_in, 16)

            def slot(s, c, t):
                if in_range(s, 0, NB):
                    dve.wait_ge(product, s + 1)
                    ge(dve, x2_set, s - 3)
                    nc.vector.tensor_tensor(part_ring[:, c], core.bank(c % 2, D), bias, ALU.add).then_inc(biased, 1)
                if in_range(s, 1, NB + 1):
                    dve.wait_ge(x_in[(c - 1) % 4], (turn(t, c, 1, 4) + 1) * 16)
                    dve.wait_ge(biased, s)
                    nc.vector.tensor_tensor(core.arena[:, cols(s - 1, D)], part_ring[:, (c - 1) % 4],
                                            x_ring[:, (c - 1) % 4], ALU.add).then_inc(x2_set, 1)
                if in_range(s, 2, NB + 2):
                    dve.wait_ge(x2_set, s - 1)
                    row_stats(nc, core, s - 2, core.arena[:, cols(s - 2, D)])
            unrolled(dve, NB + 2, 4, slot, 4, 4)
    finish_moments(nc, core, "x2")


def feature_norm(nc, core, g0, b0, table):
    CH = 7
    CHUNKS = NB // CH
    assert CHUNKS * CH == NB
    gamma, beta, mean, rstd = (core.hot[:, 2 + n // 2, (n % 2) * 512:(n % 2) * 512 + D] for n in range(4))
    squares = core.work[:, 0:2 * CH * D].rearrange("p (r n) -> p r n", r=2)

    def chunk(q):
        return core.arena[:, cols(q, CH * D)]

    def by_block(t):
        return t.rearrange("p (b n) -> p b n", b=CH)

    def wide(vec):
        return vec.unsqueeze(1).to_broadcast([P, CH, D])

    def valid(q, i):
        return TAIL if isinstance(q, int) and q == CHUNKS - 1 and i == CH - 1 else P

    with ExitStack() as st:
        (vecs_in, row_set, summed, centred, squared, square_summed, var_set, rooted, scaled, shifted) = sems(
            nc, st, "vecs_in row_set summed centred squared square_summed var_set rooted0 scaled h_shifted")
        kept = ring_sems(nc, st, "h_kept", CHUNKS)
        block = st.enter_context(nc.Block())

        @block.sync
        def _(sp):
            sp.dma_start(gamma, g0.partition_broadcast(P)).then_inc(vecs_in, 16)
            sp.dma_start(beta, b0.partition_broadcast(P)).then_inc(vecs_in, 16)
            for q in range(CHUNKS):
                sp.wait_ge(shifted, q + 1)
                sp.dma_start(table[q * CH * P:(q + 1) * CH * P, :].rearrange("(b p) n -> p b n", p=P), by_block(chunk(q)))\
                    .then_inc(kept[q], 16)
            for q in range(CHUNKS):
                sp.wait_ge(kept[q], 16)

        @block.vector
        def _(dve):
            def norm_rows(q, c, t):
                for i in range(CH):
                    rows = core.arena[:, cols(q, CH * D, i * D, D)]
                    m = core.moments[:, bass.ds(q * CH + i, 1)].rearrange("p o n -> p (o n)")
                    nc.vector.tensor_scalar(rows, rows, m[:, 0:1], m[:, 2:3], ALU.subtract, ALU.mult).then_inc(row_set, 1)

            def centre(q, c, t):
                nc.vector.tensor_tensor(by_block(chunk(q)), by_block(chunk(q)), wide(mean), ALU.subtract).then_inc(centred, 1)

            def affine(q, c, t):
                if in_range(q, 0, CHUNKS):
                    nc.vector.tensor_tensor(by_block(chunk(q)), by_block(chunk(q)), wide(rstd), ALU.mult).then_inc(scaled, 1)
                if in_range(q, 1, CHUNKS + 1):
                    dve.wait_ge(scaled, q)
                    nc.vector.tensor_tensor(by_block(chunk(q - 1)), by_block(chunk(q - 1)), wide(beta), ALU.add)\
                        .then_inc(shifted, 1)
            unrolled(dve, CHUNKS, 1, norm_rows, 1, 1)
            dve.wait_ge(summed, CHUNKS)
            nc.vector.tensor_scalar(mean, core.bank(0, D), 1.0 / N, None, ALU.mult)
            dve.drain()
            unrolled(dve, CHUNKS, 1, centre, 1, 1)
            dve.wait_ge(square_summed, CHUNKS)
            nc.vector.tensor_scalar(rstd, core.bank(1, D), 1.0 / N, EPS, ALU.mult, ALU.add).then_inc(var_set, 1)
            dve.wait_ge(rooted, 1)
            nc.vector.reciprocal(rstd, rstd)
            dve.wait_ge(vecs_in, 32)
            dve.drain()
            nc.vector.tensor_tensor(rstd, rstd, gamma, ALU.mult)
            dve.drain()
            unrolled(dve, CHUNKS + 1, 1, affine, 1, 2)

        @block.scalar
        def _(act):
            def square(q, c, t):
                act.wait_ge(centred, q + 1)
                ge(act, square_summed, q - 1)
                nc.scalar.activation(squares[:, c], chunk(q), ACT.Square).then_inc(squared, 1)
            unrolled(act, CHUNKS, 2, square, 2, 1)
            act.wait_ge(var_set, 1)
            nc.scalar.activation(rstd, rstd, ACT.Sqrt).then_inc(rooted, 1)

        @block.tensor
        def _(pe):
            def add_rows(q, c, t):
                for i in range(CH):
                    pe.wait_ge(row_set, q * CH + i + 1)
                    n = valid(q, i)
                    last = nc.tensor.matmul(core.bank(0, D), core.ones[0:n, :], core.arena[0:n, cols(q, CH * D, i * D, D)],
                                            start=isinstance(q, int) and q == 0 and i == 0,
                                            stop=isinstance(q, int) and q == CHUNKS - 1 and i == CH - 1)
                last.then_inc(summed, 1)

            def add_squares(q, c, t):
                pe.wait_ge(squared, q + 1)
                for i in range(CH):
                    n = valid(q, i)
                    last = nc.tensor.matmul(core.bank(1, D), core.ones[0:n, :], squares[0:n, c, i * D:(i + 1) * D],
                                            start=isinstance(q, int) and q == 0 and i == 0,
                                            stop=isinstance(q, int) and q == CHUNKS - 1 and i == CH - 1)
                last.then_inc(square_summed, 1)
            unrolled(pe, CHUNKS, 1, add_rows, 1, 1)
            unrolled(pe, CHUNKS, 2, add_squares, 2, 1)


def gin_layer(nc, core, name, wa, ba, gamma, beta, wb, bb, table=None, x2_rows=None):
    PAIRS = -(-NB // 2)
    w_a = core.hot[:, 0, 0:2 * D].rearrange("p (k n) -> p k n", k=2)
    w_b = core.hot[:, 0, 2 * D:4 * D].rearrange("p (k n) -> p k n", k=2)
    vecs = core.hot[:, 1, 0:6].rearrange("p (v k) -> p v k", v=3)
    bias = core.hot[:, 1, 8:8 + D]
    agg = core.hot[:, 1, 300:304].rearrange("p (k n) -> p k n", k=2)
    scale, shift, std = (core.hot[:, 1, 304 + 2 * n:306 + 2 * n] for n in range(3))
    stats = core.hot[:, 2, 0:2 * PAIRS * 6].rearrange("p (k q n) -> p k q n", k=2, q=PAIRS)
    u = core.work[:, 0:4 * D].rearrange("p (r n) -> p r n", r=4)
    ut = core.work[:, 4 * D:8 * D].rearrange("p (r k n) -> p r k n", r=2, k=2)
    rt = core.work[:, 8 * D:12 * D].rearrange("p (r k n) -> p r k n", r=2, k=2)

    def hidden(q, k, n=None):
        return core.arena[:, cols(q, 2 * D, AGG0 + k * blocks(q) * P, n or blocks(q) * P)]

    def width(q):
        return TAIL if isinstance(q, int) and q == PAIRS - 1 else D

    def blocks(q):
        return 1 if isinstance(q, int) and q == PAIRS - 1 else 2

    with ExitStack() as st:
        weights_in, u_set, u_turned, ut_copied, product, hid_set, stats_set = sems(
            nc, st, " ".join(f"{name}_{n}" for n in "weights_in u_set u_turned ut_copied product hid_set stats_set".split()))
        block = st.enter_context(nc.Block())

        @block.sync
        def _(sp):
            for t, a in ((w_a, wa.rearrange("(k p) n -> p k n", p=P)), (w_b, wb.rearrange("(k p) n -> p k n", p=P)),
                         (vecs[:, 0], ba), (vecs[:, 1], gamma),
                         (vecs[:, 2], beta), (bias, bb.partition_broadcast(P))):
                sp.dma_start(t, a).then_inc(weights_in, 16)

        @block.vector
        def _(dve):
            def slot(s, c, t):
                if in_range(s, 0, PAIRS):
                    ge(dve, u_turned, 2 * (s - 1))
                    for i in range(blocks(s)):
                        nc.vector.tensor_tensor(u[:, 2 * c + i], core.arena[:, cols(s, 2 * D, i * D, D)],
                                                core.arena[:, cols(s, 2 * ACW, AGG0 + i * ACW, D)], ALU.add)\
                            .then_inc(u_set, 1)
                if in_range(s, 2, PAIRS + 2):
                    g = s - 2
                    dve.wait_ge(hid_set, s - 1)
                    for k in range(2):
                        last = nc.vector.bn_stats(stats[:, k, bass.ds(g, 1)].rearrange("p o n -> p (o n)"),
                                                  hidden(g, k, width(g)))
                    last.then_inc(stats_set, 1)
            unrolled(dve, PAIRS + 2, 2, slot, 2, 4)
            dve.wait_ge(stats_set, PAIRS)
            for k in range(2):
                nc.vector.bn_aggr(agg[:, k], stats[:, k])
            dve.drain()
            nc.vector.tensor_scalar(std, agg[:, :, 1], EPS, None, ALU.add)

        @block.tensor
        def _(pe):
            def slot(s, c, t):
                if in_range(s, 0, PAIRS):
                    ge(pe, ut_copied, s - 1)
                    for i in range(blocks(s)):
                        pe.wait_ge(u_set, 2 * s + i + 1)
                        for k in range(2):
                            last = nc.tensor.transpose(core.bank(c)[:, k * D + i * P:k * D + (i + 1) * P],
                                                       u[:, 2 * c + i, k * P:(k + 1) * P], core.ident[:])
                        last.then_inc(u_turned, 1)
                if in_range(s, 1, PAIRS + 1):
                    r, n = (c + 1) % 2, blocks(s - 1) * P
                    if isinstance(s, int) and s == 1:
                        pe.wait_ge(weights_in, 96)
                    pe.wait_ge(ut_copied, s)
                    ge(pe, hid_set, s - 2)
                    for m in range(2):
                        for k in range(2):
                            last = nc.tensor.matmul(core.bank(2 + r)[:, m * D:m * D + n], w_a[:, k, m * P:(m + 1) * P],
                                                    ut[:, r, k, 0:n], start=(k == 0), stop=(k == 1))
                    last.then_inc(product, 1)
            unrolled(pe, PAIRS + 1, 2, slot, 4, 3)

        @block.scalar
        def _(act):
            act.wait_ge(weights_in, 96)

            def slot(s, c, t):
                if in_range(s, 0, PAIRS):
                    n = blocks(s) * P
                    act.wait_ge(u_turned, 2 * s + blocks(s))
                    ge(act, product, s - 1)
                    nc.scalar.activation(ut[:, c, :, 0:n], core.bank(c).rearrange("p (k n) -> p k n", k=2)[:, :, 0:n],
                                         ACT.Copy).then_inc(ut_copied, 1)
                if in_range(s, 1, PAIRS + 1):
                    n = blocks(s - 1) * P
                    act.wait_ge(product, s)
                    for m in range(2):
                        last = nc.scalar.activation(hidden(s - 1, m), core.bank(2 + (c + 1) % 2)[:, m * D:m * D + n],
                                                    ACT.Identity, bias=vecs[:, 0, m:m + 1])
                    last.then_inc(hid_set, 1)
            unrolled(act, PAIRS + 1, 2, slot, 2, 3)

    with ExitStack() as st:
        rooted, affine_set, r_set, product, biased, out_set = sems(
            nc, st, " ".join(f"{name}_{n}" for n in "rooted affine_set r_set product2 biased out_set".split()))
        moved = ring_sems(nc, st, f"{name}_moved", 2)
        block = st.enter_context(nc.Block())

        @block.sync
        def _(sp):
            def slot(q, c, t):
                n = blocks(q)
                if table is not None:
                    sp.wait_ge(out_set, q + 1)
                    pair, rows = core.arena[:, cols(q, 2 * D, 0, n * D)], table
                else:
                    sp.wait_ge(r_set, q + 1)
                    pair, rows = core.arena[:, cols(q, 2 * D, AGG0, n * D)], x2_rows
                sp.nop(nofuse=True)
                rows = rows[bass.ds(q * 2 * P, n * P), :].rearrange("(b p) n -> p b n", p=P)
                pair = pair.rearrange("p (b n) -> p b n", b=n)
                ge(sp, moved[c], t * 16)
                ends = (rows, pair) if table is not None else (pair, rows)
                sp.dma_start(*ends).then_inc(moved[c], 16)
            unrolled(sp, PAIRS, 2, slot, 2, 3)
            for r in range(2):
                sp.wait_ge(moved[r], 16 * ((PAIRS + 1 - r) // 2))

        @block.scalar
        def _(act):
            nc.scalar.activation(std, std, ACT.Sqrt).then_inc(rooted, 1)
            act.wait_ge(affine_set, 1)

            def slot(s, c, t):
                if in_range(s, 0, PAIRS):
                    n = blocks(s) * P
                    ge(act, product, 2 * (s - 1))
                    for k in range(2):
                        last = nc.scalar.activation(rt[:, c, k, 0:n], hidden(s, k), ACT.Relu,
                                                    scale=scale[:, k:k + 1], bias=shift[:, k:k + 1])
                    last.then_inc(r_set, 1)
                if in_range(s, 1, PAIRS + 1):
                    for i in range(blocks(s - 1)):
                        act.wait_ge(biased, 2 * (s - 1) + i + 1)
                        out = core.arena[:, cols(s - 1, 2 * D, i * D, D)]
                        last = nc.scalar.activation(out, out, ACT.Relu)
                    last.then_inc(out_set, 1)
            unrolled(act, PAIRS + 1, 2, slot, 2, 3)

        @block.vector
        def _(dve):
            dve.wait_ge(rooted, 1)
            nc.vector.reciprocal(scale, std)
            dve.drain()
            nc.vector.tensor_tensor(scale, scale, vecs[:, 1], ALU.mult)
            dve.drain()
            nc.vector.tensor_tensor(shift, scale, agg[:, :, 0], ALU.mult)
            dve.drain()
            nc.vector.tensor_tensor(shift, vecs[:, 2], shift, ALU.subtract).then_inc(affine_set, 1)

            def slot(s, c, t):
                for i in range(blocks(s)):
                    dve.wait_ge(product, 2 * s + i + 1)
                    nc.vector.tensor_tensor(core.arena[:, cols(s, 2 * D, i * D, D)], core.bank(2 * c + i, D), bias, ALU.add)\
                        .then_inc(biased, 1)
            unrolled(dve, PAIRS, 2, slot, 2, 3)

        @block.tensor
        def _(pe):
            def slot(s, c, t):
                pe.wait_ge(r_set, s + 1)
                ge(pe, biased, 2 * (s - 1))
                for i in range(blocks(s)):
                    for k in range(2):
                        last = nc.tensor.matmul(core.bank(2 * c + i, D), rt[:, c, k, i * P:(i + 1) * P], w_b[:, k],
                                                start=(k == 0), stop=(k == 1))
                    last.then_inc(product, 1)
            unrolled(pe, PAIRS, 2, slot, 2, 3)


def output_rows(nc, core, weight_t, bias, out):
    w = core.hot[:, 0, 0:2 * D].rearrange("p (k n) -> p k n", k=2)
    b_wide = core.hot[:, 1, 0:D]
    rows = core.work[:, 8 * D:12 * D].rearrange("p (r n) -> p r n", r=4)
    with ExitStack() as st:
        weights_in, = sems(nc, st, "out_weights_in")
        block = st.enter_context(nc.Block())

        @block.sync
        def _(sp):
            sp.dma_start(w, weight_t.rearrange("(k p) n -> p k n", p=P)).then_inc(weights_in, 16)
            sp.dma_start(b_wide, bias.partition_broadcast(P)).then_inc(weights_in, 16)
            sp.wait_ge(weights_in, 32)

    def place(s):
        return core.arena[:, cols(s, D, AGG0)]

    def add_rows(s, r):
        return nc.vector.tensor_tensor(place(s), place(s), core.arena[:, cols(s, D)], ALU.add)

    row_moments(nc, core, "x3", (add_rows,), place)

    def prepare(dve, s, tile):
        return normalized(nc, core, tile, place(s), s)

    def finish(dve, s, prod, r):
        nc.vector.tensor_tensor(rows[:, r], prod, b_wide, ALU.add)
        dve.drain()
        return nc.vector.tensor_tensor(rows[:, r], rows[:, r], place(s), ALU.add)

    def store(sp, s, r):
        n = TAIL if isinstance(s, int) and s == NB - 1 else P
        return sp.dma_start(out[bass.ds(s * P, n), :], rows[0:n, r])

    dense_tiles(nc, "out", core, [w[:, 0], w[:, 1]], D, prepare, finish, store)


def gnn_program(nc, a, out):
    def dram(name, width):
        return nc.dram_tensor(name, (NPAD, width), F32).ap()

    rows1, rows2, rows3 = dram("rows_gat1", ROW1), dram("rows_gat2", ROW2), dram("rows_gin", D)
    rows4, x1_rows, x2_rows = dram("rows_gin2", D), dram("x1_rows", D), dram("x2_rows", D)
    with ExitStack() as st:
        core = Core(nc, st)
        set_constants(nc, core)
        plan_steps(nc, core, a["src"], a["dst"])
        gat1_tables(nc, core, a["x"], a["L0_gnn_W1"], a["L0_gnn_al1"], a["L0_gnn_ar1"], rows1)
        spread_attention(nc, core, H1)
        edge_pass(nc, core, "e1", rows1, ROW1, H1, True)
        gat2_tables(nc, core, a["L0_gnn_W2"], a["L0_gnn_al2"], a["L0_gnn_ar2"], a["L0_gnn_b1"], rows2)
        spread_attention(nc, core, 1)
        edge_pass(nc, core, "e2", rows2, ROW2, 1, True)
        first_residual(nc, core, a["x"], a["L0_gnn_b2"], x1_rows)
        wl = core.hot[:, 0].rearrange("p (k n) -> p k n", k=2)
        bl = core.hot[:, 1, 0:NH * NSL]
        slice_logits(nc, core, a["w_xt"], a["b_xt"], a["L0_ffn_W_slice"], a["L0_ffn_b_slice"], a["temperature"], wl, bl)
        total = slice_weights(nc, core, wl, bl)
        v2 = core.hot[:, 0].rearrange("p (j n) -> p j n", j=NH // 2)
        slice_attention(nc, core, total, a["L0_ffn_W_fx"], a["b_fxt"], a["L0_ffn_W_q"], a["L0_ffn_W_k"], a["L0_ffn_W_v"],
                        a["L0_ffn_W_out"], v2)
        second_residual(nc, core, v2, a["L0_ffn_b_out"], x1_rows, x2_rows)
        feature_norm(nc, core, a["L1_gnn_g0"], a["L1_gnn_b0"], rows3)
        edge_pass(nc, core, "e3", rows3, D, 1, False)
        gin_layer(nc, core, "n1", *(a["L1_gnn_" + n] for n in ("W1a", "b1a", "g1", "bt1", "W1b", "b1b")), table=rows4)
        edge_pass(nc, core, "e4", rows4, D, 1, False)
        gin_layer(nc, core, "n2", *(a["L1_gnn_" + n] for n in ("W2a", "b2a", "g2", "bt2", "W2b", "b2b")), x2_rows=x2_rows)
        output_rows(nc, core, a["weight_t"], a["L1_ffn_bias"], out)


def kernel(**inputs):
    import concourse.bacc as bacc
    from concourse.bass_utils import run_bass_kernel_spmd

    nc = bacc.Bacc("TRN2", target_bir_lowering=False, num_devices=1)
    laid = {n: np.asarray(v) for n, v in inputs.items()}
    laid["w_xt"] = laid.pop("L0_ffn_W_x").T
    laid["b_xt"] = laid.pop("L0_ffn_b_x").reshape(NH, DH).T
    laid["b_fxt"] = laid.pop("L0_ffn_b_fx").reshape(NH, DH).T
    laid["temperature"] = laid.pop("L0_ffn_temperature").reshape(NH)
    laid["weight_t"] = laid.pop("L1_ffn_weight").T
    for n in "b1a g1 bt1 b2a g2 bt2".split():
        laid["L1_gnn_" + n] = laid["L1_gnn_" + n].reshape(D // P, P).T
    arrays, views = {}, {}
    for name, value in laid.items():
        arrays[name] = np.ascontiguousarray(value)
        views[name] = nc.dram_tensor(name, value.shape, mybir.dt.from_np(value.dtype), kind="ExternalInput").ap()
    out = nc.dram_tensor("out", (N, D), F32, kind="ExternalOutput").ap()
    gnn_program(nc, views, out)
    result = run_bass_kernel_spmd(nc, [arrays], core_ids=[0])
    return result.results[0]["out"]
```
